# Optimizing a Trainium2 kernel written in Bass

```python
import numpy as np
import jax
import jax.numpy as jnp

def _softmax(x, axis=-1):
    return jax.nn.softmax(x, axis=axis)

def _gelu(x):
    return jax.nn.gelu(x, approximate=True)

def _silu(x):
    return jax.nn.silu(x)

def _sigmoid(x):
    return jax.nn.sigmoid(x)

def _layernorm(x, axis=-1, eps=1e-05):
    m = jnp.mean(x, axis=axis, keepdims=True)
    v = jnp.var(x, axis=axis, keepdims=True)
    return (x - m) / jnp.sqrt(v + eps)

def _scatter_add(tgt, idx, src, axis=0):
    return tgt.at[idx].add(src)

def _segment_sum(src, seg, n):
    return jax.ops.segment_sum(src, seg, n)
kernel_name = 'mk_gnn_resnorm_d2_gnn_r8_8c7efd'

def setup_inputs(seed: int=0):
    np.random.seed(seed)
    _w = jnp.asarray

    def _rec_inputs():
        import jax
        import jax.numpy as jnp
        _gk = jax.random.key(seed)
        x = -0.000202 + 1 * jax.random.normal(jax.random.fold_in(_gk, 1), (6250, 160), jnp.float32)
        src = jax.random.randint(jax.random.fold_in(_gk, 2), (200000,), 0, 6250, jnp.int32)
        dst = jax.random.randint(jax.random.fold_in(_gk, 3), (200000,), 0, 6250, jnp.int32)
        _o = jnp.argsort(dst, stable=True)
        src = src[_o]
        dst = dst[_o]
        edge_attr_4 = -0.000414295 + 0.999828 * jax.random.normal(jax.random.fold_in(_gk, 12), (200000, 4), jnp.float32)
        edge_attr_8 = jax.random.uniform(jax.random.fold_in(_gk, 13), (200000, 8), jnp.float32, 0.0, 1)
        node_vec1 = jax.random.uniform(jax.random.fold_in(_gk, 15), (6250, 1), jnp.float32, 0.0, 1)
        return (x, src, dst, edge_attr_4, edge_attr_8, node_vec1)
    x, src, dst, edge_attr_4, edge_attr_8, node_vec1 = _rec_inputs()

    def _L0_gnn_setup():
        import jax, jax.numpy as jnp
        import numpy as np
        N = 5000
        E = 50000
        MUL0, MUL1 = (64, 32)
        RAD, HID = (8, 64)
        WNUM = 192
        NUM_NEIGHBORS = 10.0
        INV3 = 1.0 / np.sqrt(3.0)

        def _lin(s, v, Ws, Wv, attr):
            out_s = s @ Ws * attr * (1.0 / np.sqrt(Ws.shape[0]))
            out_v = jnp.einsum('nud,uv->nvd', v, Wv) * attr[..., None] * (1.0 / np.sqrt(Wv.shape[0]))
            return (out_s, out_v)
        key = jax.random.key(seed)
        ks = jax.random.split(key, 16)
        return {'node_input': jax.random.normal(ks[0], (N, MUL0 + 3 * MUL1), jnp.float32), 'node_attr': jnp.ones((N, 1), jnp.float32), 'edge_attr': jax.random.normal(ks[1], (E, 4), jnp.float32), 'edge_scalars': jax.random.uniform(ks[2], (E, RAD), jnp.float32), 'W_sc_s': jax.random.normal(ks[3], (MUL0, MUL0), jnp.float32), 'W_sc_v': jax.random.normal(ks[4], (MUL1, MUL1), jnp.float32), 'W1_s': jax.random.normal(ks[5], (MUL0, MUL0), jnp.float32), 'W1_v': jax.random.normal(ks[6], (MUL1, MUL1), jnp.float32), 'W2_s': jax.random.normal(ks[7], (MUL0 + MUL1, MUL0), jnp.float32), 'W2_v': jax.random.normal(ks[8], (MUL0 + MUL1, MUL1), jnp.float32), 'W3': jax.random.normal(ks[9], (MUL0 + MUL1, 1), jnp.float32), 'fcW1': jax.random.normal(ks[10], (RAD, HID), jnp.float32), 'fcW2': jax.random.normal(ks[11], (HID, WNUM), jnp.float32), 'edge_src': jax.random.randint(ks[12], (E,), 0, N, jnp.int32), 'edge_dst': jax.random.randint(ks[13], (E,), 0, N, jnp.int32)}
    _L0_gnn_all = _L0_gnn_setup()
    _L0_gnn_in = {k: v for k, v in _L0_gnn_all.items() if k in ('W_sc_s', 'W_sc_v', 'W1_s', 'W1_v', 'W2_s', 'W2_v', 'W3', 'fcW1', 'fcW2')}
    del _L0_gnn_all

    def _L1_gnn_setup():
        import jax, jax.numpy as jnp
        import numpy as np
        N, E = (6250, 100000)
        MUL0, MUL1 = (64, 32)
        D = MUL0 + 3 * MUL1
        INV3 = float(1.0 / np.sqrt(3.0))
        INV6 = float(1.0 / np.sqrt(6.0))
        C0 = float(1.0 / np.sqrt(MUL0 + MUL1))
        C1 = float(np.sqrt(3.0 / (MUL0 + 2 * MUL1)))
        LIN_S = float(1.0 / np.sqrt(MUL0))
        LIN_V = float(1.0 / np.sqrt(MUL1))
        key = jax.random.key(seed)
        ks = jax.random.split(key, 10)
        x = jax.random.normal(ks[0], (N, D), dtype=jnp.float32)
        sh = jax.random.normal(ks[1], (E, 4), dtype=jnp.float32)
        edge_index = jax.random.randint(ks[2], (2, E), 0, N, dtype=jnp.int64)
        W1 = jax.random.normal(ks[3], (MUL0, MUL0), dtype=jnp.float32)
        W2 = jax.random.normal(ks[4], (MUL1, MUL0), dtype=jnp.float32)
        W3 = jax.random.normal(ks[5], (MUL0, MUL1), dtype=jnp.float32)
        W4 = jax.random.normal(ks[6], (MUL1, MUL1), dtype=jnp.float32)
        W5 = jax.random.normal(ks[7], (MUL1, MUL1), dtype=jnp.float32)
        Ws = jax.random.normal(ks[8], (MUL0, MUL0), dtype=jnp.float32)
        Wv = jax.random.normal(ks[9], (MUL1, MUL1), dtype=jnp.float32)
        return {'x': x, 'sh': sh, 'W1': W1, 'W2': W2, 'W3': W3, 'W4': W4, 'W5': W5, 'Ws': Ws, 'Wv': Wv, 'edge_index': edge_index}
    _L1_gnn_all = _L1_gnn_setup()
    _L1_gnn_in = {k: v for k, v in _L1_gnn_all.items() if k in ('W1', 'W2', 'W3', 'W4', 'W5', 'Ws', 'Wv')}
    del _L1_gnn_all
    return {'x': x, 'src': src, 'dst': dst, 'edge_attr_4': edge_attr_4, 'edge_attr_8': edge_attr_8, 'node_vec1': node_vec1, 'L0_gnn_W_sc_s': _L0_gnn_in['W_sc_s'], 'L0_gnn_W_sc_v': _L0_gnn_in['W_sc_v'], 'L0_gnn_W1_s': _L0_gnn_in['W1_s'], 'L0_gnn_W1_v': _L0_gnn_in['W1_v'], 'L0_gnn_W2_s': _L0_gnn_in['W2_s'], 'L0_gnn_W2_v': _L0_gnn_in['W2_v'], 'L0_gnn_W3': _L0_gnn_in['W3'], 'L0_gnn_fcW1': _L0_gnn_in['fcW1'], 'L0_gnn_fcW2': _L0_gnn_in['fcW2'], 'L1_gnn_W1': _L1_gnn_in['W1'], 'L1_gnn_W2': _L1_gnn_in['W2'], 'L1_gnn_W3': _L1_gnn_in['W3'], 'L1_gnn_W4': _L1_gnn_in['W4'], 'L1_gnn_W5': _L1_gnn_in['W5'], 'L1_gnn_Ws': _L1_gnn_in['Ws'], 'L1_gnn_Wv': _L1_gnn_in['Wv']}

def reference(x, src, dst, edge_attr_4, edge_attr_8, node_vec1, L0_gnn_W_sc_s, L0_gnn_W_sc_v, L0_gnn_W1_s, L0_gnn_W1_v, L0_gnn_W2_s, L0_gnn_W2_v, L0_gnn_W3, L0_gnn_fcW1, L0_gnn_fcW2, L1_gnn_W1, L1_gnn_W2, L1_gnn_W3, L1_gnn_W4, L1_gnn_W5, L1_gnn_Ws, L1_gnn_Wv):
    import jax
    import jax.numpy as jnp

    def _L0_gnn_ref(node_input, node_attr, edge_attr, edge_scalars, W_sc_s, W_sc_v, W1_s, W1_v, W2_s, W2_v, W3, fcW1, fcW2, edge_src, edge_dst):
        import jax, jax.numpy as jnp
        import numpy as np
        N = 5000
        E = 50000
        MUL0, MUL1 = (64, 32)
        RAD, HID = (8, 64)
        WNUM = 192
        NUM_NEIGHBORS = 10.0
        INV3 = 1.0 / np.sqrt(3.0)

        def _lin(s, v, Ws, Wv, attr):
            out_s = s @ Ws * attr * (1.0 / np.sqrt(Ws.shape[0]))
            out_v = jnp.einsum('nud,uv->nvd', v, Wv) * attr[..., None] * (1.0 / np.sqrt(Wv.shape[0]))
            return (out_s, out_v)
        n = node_input.shape[0]
        s_in = node_input[:, :MUL0]
        v_in = node_input[:, MUL0:].reshape(n, MUL1, 3)
        sc_s, sc_v = _lin(s_in, v_in, W_sc_s, W_sc_v, node_attr)
        f_s, f_v = _lin(s_in, v_in, W1_s, W1_v, node_attr)
        h = jax.nn.silu(edge_scalars @ fcW1 * (1.0 / np.sqrt(RAD)))
        w = h @ fcW2 * (1.0 / np.sqrt(HID))
        wA, wB, wC, wD = (w[:, :64], w[:, 64:128], w[:, 128:160], w[:, 160:192])
        xs = f_s[edge_src]
        xv = f_v[edge_src]
        y0 = edge_attr[:, :1]
        y1 = edge_attr[:, 1:4]
        outA = wA * xs * y0
        outD = wD * jnp.einsum('eud,ed->eu', xv, y1) * INV3
        outB = wB[:, :, None] * xs[:, :, None] * y1[:, None, :]
        outC = wC[:, :, None] * xv * y0[:, :, None]
        edge_feat = jnp.concatenate([outA, outD, outB.reshape(-1, MUL0 * 3), outC.reshape(-1, MUL1 * 3)], axis=1)
        agg = jax.ops.segment_sum(edge_feat, edge_dst, num_segments=n)
        agg = agg * (1.0 / np.sqrt(NUM_NEIGHBORS))
        ms = agg[:, :MUL0 + MUL1]
        mv = agg[:, MUL0 + MUL1:].reshape(n, MUL0 + MUL1, 3)
        c_s, c_v = _lin(ms, mv, W2_s, W2_v, node_attr)
        conv = jnp.concatenate([c_s, c_v.reshape(n, -1)], axis=1)
        sc = jnp.concatenate([sc_s, sc_v.reshape(n, -1)], axis=1)
        angle = 0.1 * (ms @ W3) * node_attr * (1.0 / np.sqrt(MUL0 + MUL1))
        cos, sin = (jnp.cos(angle), jnp.sin(angle))
        return cos * sc + sin * conv

    def _L1_gnn_ref(x, sh, W1, W2, W3, W4, W5, Ws, Wv, edge_index):
        import jax, jax.numpy as jnp
        import numpy as np
        N, E = (6250, 100000)
        MUL0, MUL1 = (64, 32)
        D = MUL0 + 3 * MUL1
        INV3 = float(1.0 / np.sqrt(3.0))
        INV6 = float(1.0 / np.sqrt(6.0))
        C0 = float(1.0 / np.sqrt(MUL0 + MUL1))
        C1 = float(np.sqrt(3.0 / (MUL0 + 2 * MUL1)))
        LIN_S = float(1.0 / np.sqrt(MUL0))
        LIN_V = float(1.0 / np.sqrt(MUL1))
        n = x.shape[0]
        src, dst = (edge_index[0], edge_index[1])
        s = x[:, :MUL0]
        v = x[:, MUL0:].reshape(n, MUL1, 3)
        ss, vv = (s[src], v[src])
        e0 = sh[:, 0:1]
        e1 = sh[:, 1:4]
        dot = jnp.einsum('eui,ei->eu', vv, e1)
        out0 = C0 * (ss * e0 @ W1 + dot * INV3 @ W2)
        p3 = (ss @ W3)[:, :, None] * e1[:, None, :] * INV3
        p4 = jnp.einsum('eui,uw->ewi', vv * e0[:, :, None], W4) * INV3
        p5 = jnp.einsum('eui,uw->ewi', jnp.cross(vv, e1[:, None, :]), W5) * INV6
        out1 = C1 * (p3 + p4 + p5)
        m = jnp.concatenate([out0, out1.reshape(-1, 3 * MUL1)], axis=1)
        m_agg = jax.ops.segment_sum(m, dst, num_segments=n)
        hs = m_agg[:, :MUL0] @ Ws * LIN_S
        hv = jnp.einsum('nui,uw->nwi', m_agg[:, MUL0:].reshape(n, MUL1, 3), Wv) * LIN_V
        h = jnp.concatenate([hs, hv.reshape(n, 3 * MUL1)], axis=1)
        return x + jax.nn.relu(h)
    edge_index = jnp.stack([src, dst])
    x = _layernorm(x + _L0_gnn_ref(x, node_vec1, edge_attr_4, edge_attr_8, L0_gnn_W_sc_s, L0_gnn_W_sc_v, L0_gnn_W1_s, L0_gnn_W1_v, L0_gnn_W2_s, L0_gnn_W2_v, L0_gnn_W3, L0_gnn_fcW1, L0_gnn_fcW2, src, dst), axis=-1)
    x = _layernorm(x + _L1_gnn_ref(x, edge_attr_4, L1_gnn_W1, L1_gnn_W2, L1_gnn_W3, L1_gnn_W4, L1_gnn_W5, L1_gnn_Ws, L1_gnn_Wv, edge_index), axis=-1)
    return x

_drawn_inputs = setup_inputs


def setup_inputs(seed=0):
    import zlib

    import numpy as np

    out = dict(_drawn_inputs(seed))
    spreads = {}
    factors = {'edge_attr_8': 8.0,
     'L0_gnn_W1_s': 8.0,
     'L0_gnn_W1_v': 8.0,
     'L0_gnn_W2_s': 8.0,
     'L0_gnn_W2_v': 8.0,
     'L0_gnn_W3': 8.0,
     'L0_gnn_fcW1': 8.0,
     'L0_gnn_fcW2': 8.0,
     'L0_gnn_W_sc_s': 23.13,
     'L0_gnn_W_sc_v': 27.885}
    for name, (base, spread) in spreads.items():
        noise = np.random.default_rng([zlib.crc32(name.encode()), seed]).standard_normal(out[name].shape)
        drawn = base * np.exp(spread * noise) if base else spread * noise
        out[name] = jnp.asarray(drawn.astype(out[name].dtype))
    for name, factor in factors.items():
        out[name] = (out[name] * factor).astype(out[name].dtype)
    return out
```

```python
from contextlib import ExitStack

import numpy as np

import concourse.bass as bass
from concourse import mybir

ALU = mybir.AluOpType
ACT = mybir.ActivationFunctionType
F32 = mybir.dt.float32
I32 = mybir.dt.int32
AX = mybir.AxisListType

P = 128
NODES, EDGES = 6250, 200000
MUL0, MUL1 = 64, 32
D = MUL0 + 3 * MUL1
NY = 4
RAD, HID = 8, 64
WNUM = 2 * MUL0 + 2 * MUL1

CH = 7
CHUNK = CH * P
NCH = -(-EDGES // CHUNK)
assert NCH % 2 == 0
TILES = NCH * CH
EPAD = TILES * P
WIN = P // NY

G = 5
NG = 10
NT = G * NG
NPAD = NT * P
assert NPAD >= NODES + WIN

PROD = 2 * D
BLK = MUL1 + D
OUT0 = 1 + D
SLOT = 256

INV3, INV6 = 1 / np.sqrt(3.0), 1 / np.sqrt(6.0)
MIX = 1 / np.sqrt(MUL0 + MUL1)
C1 = np.sqrt(3.0 / (MUL0 + 2 * MUL1))
LIN_S, LIN_V = 1 / np.sqrt(MUL0), 1 / np.sqrt(MUL1)
NEIGHBORS = 10.0
EPS = 1e-5

TURN = 2 * np.pi
TURN_HI = 6.28125
TURN_MID = float(np.float32(TURN - TURN_HI))
TURN_LO = float(TURN - TURN_HI - TURN_MID)
ROUND = 1.5 * 2.0**23
PI_IN = 3.1415925


def load_and_embed(nc, io, keep):
    with ExitStack() as ctx:
        def sb(name, shape, dt=F32):
            return ctx.enter_context(nc.sbuf_tensor(name, shape, dt))

        def sem(name):
            return ctx.enter_context(nc.semaphore(name))

        xs_t = sb("xs_t", [MUL0, 2, G * P])
        xv_t = sb("xv_t", [MUL1, 2, 3, G * P])
        node_ws = sb("node_ws", [MUL0, 2 * MUL0])
        node_wv = sb("node_wv", [MUL1, 2 * MUL1])
        pre_s = sb("pre_s", [MUL0, MUL0 + MUL1 + MUL0])
        pre_v = sb("pre_v", [MUL1, MUL0 + 2 * MUL1 + MUL1])
        src_rows = sb("src_rows", [P, NT, D])
        zeros = sb("zeros", [P, 3200])
        dst_int = sb("dst_int", [P, TILES], I32)
        dst_chunks = sb("dst_chunks", [NCH // 2, 2, CHUNK], I32)
        range_rows = sb("range_rows", [NCH // 2, 2, 2], I32)
        banks = ctx.enter_context(nc.psum_tensor("embed_banks", [P, G, 512], F32))
        pre_bank = ctx.enter_context(nc.psum_tensor("pre_bank", [P, 2, 512], F32))

        weights_in = sem("weights_in")
        weights_scaled = sem("weights_scaled")
        attr_in = sem("attr_in")
        xt_in = [sem("xt_in0"), sem("xt_in1")]
        embedded = sem("embedded")
        rows_out = sem("rows_out")
        self_out = sem("self_out")
        rows_stored = sem("rows_stored")
        zeros_made = sem("zeros_made")
        zeros_stored = sem("zeros_stored")
        chunks_in = sem("chunks_in")
        ranges_made = sem("ranges_made")
        ranges_stored = sem("ranges_stored")
        ranges_in = sem("ranges_in")
        dst_in = sem("dst_in")
        rest_in = sem("rest_in")
        premul = sem("premul")
        N_WEIGHTS = 4 + 2 + 3 + 4 + 4 + 2
        block = ctx.enter_context(nc.Block())

        @block.sync
        def _(sp):
            def load_columns(g, h):
                cols = bass.ds(g * (G * P), G * P)
                sp.dma_start(xs_t[:, h, :], io["x_t"][0:MUL0, cols]).then_inc(xt_in[h], 16)
                sp.dma_start(xv_t[:, h, :, :],
                             io["x_t"][MUL0:D, :].rearrange("(i u) n -> u i n", i=3)[:, :, cols]
                             ).then_inc(xt_in[h], 16)

            for dst, src in (
                (node_ws[:, 0:MUL0], io["L0_gnn_W1_s"]), (node_ws[:, MUL0:], io["L0_gnn_W_sc_s"]),
                (node_wv[:, 0:MUL1], io["L0_gnn_W1_v"]), (node_wv[:, MUL1:], io["L0_gnn_W_sc_v"]),
            ):
                sp.dma_start(dst, src).then_inc(weights_in, 16)
            load_columns(0, 0)
            load_columns(1, 1)
            sp.dma_start(keep["attr"][:], io["attr"]).then_inc(attr_in, 16)
            rest_s, rest_v = MUL0, MUL0
            for dst, src in (
                (keep["fc1"][:], io["L0_gnn_fcW1"]), (keep["fc2"][:], io["L0_gnn_fcW2"]),
                (keep["out_s"][0:MUL1, 1:], io["L0_gnn_W2_s"][rest_s:, :]),
                (keep["out_s"][MUL1:, 1:], io["L0_gnn_W2_s"][0:MUL0, :]),
                (keep["out_s"][0:MUL1, 0:1], io["L0_gnn_W3"][rest_s:, :]),
                (keep["out_s"][MUL1:, 0:1], io["L0_gnn_W3"][0:MUL0, :]),
                (keep["out_v"][0:MUL1, :], io["L0_gnn_W2_v"][rest_v:, :]),
                (keep["out_v"][MUL1:, :], io["L0_gnn_W2_v"][0:MUL0, :]),
                (pre_s[:, 0:MUL0 + MUL1], io["mix_s_t"]), (pre_s[:, MUL0 + MUL1:], io["L1_gnn_Ws"]),
                (pre_v[:, 0:MUL0 + 2 * MUL1], io["mix_v_t"]), (pre_v[:, MUL0 + 2 * MUL1:], io["L1_gnn_Wv"]),
                (keep["node_of_column"][:], io["node_of_column"]), (keep["identity"][:], io["identity"]),
                (keep["harmonic_mask"][:], io["harmonic_mask"]),
            ):
                sp.dma_start(dst, src).then_inc(weights_in, 16)

            def store_rows(g):
                sp.wait_ge(rows_out, (g + 1) * G)
                sp.dma_start(keep["src_table"].rearrange("(t p) f -> p t f", p=P)[:, bass.ds(g * G, G), :],
                             src_rows[:, bass.ds(g * G, G), :]).then_inc(rows_stored, 16)

            with sp.Fori(0, NG // 2 - 1) as i:
                for h in range(2):
                    store_rows(i * 2 + h)
                    sp.wait_ge(embedded, (i * 2 + h + 1) * G)
                    load_columns(i * 2 + h + 2, h)
            for g in (NG - 2, NG - 1):
                store_rows(g)
            sp.wait_ge(rows_stored, 16 * NG)

        @block.tensor
        def _(pe):
            pe.wait_ge(weights_scaled, 2)
            with pe.Fori(0, NG // 2) as i:
                for h in range(2):
                    pe.wait_ge(xt_in[h], i * 32 + 32)
                    for t in range(G):
                        n = (i * 2 + h) * G + t
                        pe.wait_ge(self_out, n + 1)
                        cols = slice(t * P, t * P + P)
                        pe.matmul(banks[:, t, 0:2 * MUL0], xs_t[:, h, cols], node_ws[:], start=True, stop=True)
                        for c in range(3):
                            at = 2 * MUL0 + c * 2 * MUL1
                            mm = pe.matmul(banks[:, t, at:at + 2 * MUL1], xv_t[:, h, c, cols], node_wv[:],
                                           start=True, stop=True)
                        mm.then_inc(embedded, 1)
            pe.wait_ge(weights_in, 16 * N_WEIGHTS)
            pe.matmul(pre_bank[0:MUL0 + MUL1, 0, 0:MUL0], pre_s[:, 0:MUL0 + MUL1], pre_s[:, MUL0 + MUL1:],
                      start=True, stop=True)
            pe.matmul(pre_bank[:, 1, 0:MUL1], pre_v[:, 0:MUL0 + 2 * MUL1], pre_v[:, MUL0 + 2 * MUL1:],
                      start=True, stop=True).then_inc(premul, 1)

        @block.scalar
        def _(act):
            act.wait_ge(attr_in, 16)
            with act.Fori(0, NG) as g:
                for t in range(G):
                    n = g * G + t
                    act.wait_ge(embedded, n + 1)
                    scale = keep["attr"][:, bass.ds(n, 1)]
                    nc.scalar.activation(src_rows[:, bass.ds(n, 1), 0:MUL0].rearrange("p t f -> p (t f)"),
                                         banks[:, t, 0:MUL0], ACT.Copy, scale=scale)
                    nc.scalar.activation(
                        src_rows[:, bass.ds(n, 1), MUL0:].rearrange("p t (c f) -> p (t c) f", c=3),
                        banks[:, t, 2 * MUL0:2 * MUL0 + 6 * MUL1].rearrange("p (c f) -> p c f", c=3)[:, :, 0:MUL1],
                        ACT.Copy, scale=scale).then_inc(rows_out, 1)

        @block.vector
        def _(dve):
            nc.vector.memset(zeros[:], 0.0).then_inc(zeros_made, 1)
            dve.sem_inc(self_out, G)
            dve.wait_ge(weights_in, 16 * 19)
            nc.vector.tensor_scalar(node_ws[:], node_ws[:], float(LIN_S), None, ALU.mult).then_inc(weights_scaled, 1)
            nc.vector.tensor_scalar(node_wv[:], node_wv[:], float(LIN_V), None, ALU.mult).then_inc(weights_scaled, 1)
            nc.vector.tensor_scalar(keep["fc2"][:], keep["fc2"][:], float(1 / np.sqrt(HID)), None, ALU.mult)
            out_scale = float(MIX / np.sqrt(NEIGHBORS))
            nc.vector.tensor_scalar(keep["out_v"][:], keep["out_v"][:], out_scale, None, ALU.mult)
            nc.vector.tensor_scalar(keep["out_s"][:], keep["out_s"][:], out_scale, None, ALU.mult)
            dve.drain()
            nc.vector.tensor_scalar(keep["out_s"][0:MUL1, :], keep["out_s"][0:MUL1, :], float(INV3), None, ALU.mult)
            dve.drain()
            nc.vector.tensor_scalar(keep["out_s"][:, 0:1], keep["out_s"][:, 0:1], 0.1, None, ALU.mult)
            dve.wait_ge(attr_in, 16)
            with dve.Fori(0, NG) as g:
                for t in range(G):
                    n = g * G + t
                    dve.wait_ge(embedded, n + 1)
                    dve.wait_ge(rows_out, n + 1)
                    scale = keep["attr"][:, bass.ds(n, 1)]
                    row = keep["sc"][:, bass.ds(n, 1), :].rearrange("p t f -> p (t f)")
                    nc.vector.tensor_scalar(row[:, 0:MUL0], banks[:, t, MUL0:2 * MUL0], scale, None, ALU.mult)
                    nc.vector.tensor_scalar(
                        row[:, MUL0:].rearrange("p (w c) -> p c w", c=3),
                        banks[:, t, 2 * MUL0:2 * MUL0 + 6 * MUL1].rearrange("p (c f) -> p c f", c=3)[:, :, MUL1:],
                        scale, None, ALU.mult).then_inc(self_out, 1)
            dve.wait_ge(chunks_in, 16)
            nc.vector.tensor_reduce(range_rows[:, :, 0], dst_chunks[:], AX.X, ALU.min)
            nc.vector.tensor_reduce(range_rows[:, :, 1], dst_chunks[:], AX.X, ALU.max).then_inc(ranges_made, 1)
            dve.wait_ge(dst_in, 16)
            nc.vector.tensor_copy(keep["dst"][:], dst_int[:])
            dve.wait_ge(premul, 1)
            nc.vector.tensor_scalar(keep["mix_s"][:], pre_bank[0:MUL0 + MUL1, 0, 0:MUL0],
                                    float(MIX * LIN_S), None, ALU.mult)
            nc.vector.tensor_scalar(keep["mix_v"][:], pre_bank[:, 1, 0:MUL1],
                                    float(C1 * INV3 * LIN_V), None, ALU.mult)
            dve.drain()
            nc.vector.tensor_scalar(keep["mix_s"][MUL0:, :], keep["mix_s"][MUL0:, :], float(INV3), None, ALU.mult)
            nc.vector.tensor_scalar(keep["mix_v"][MUL0 + MUL1:, :], keep["mix_v"][MUL0 + MUL1:, :],
                                    float(INV6 / INV3), None, ALU.mult)
            dve.wait_ge(ranges_in, 16)
            nc.vector.tensor_copy(keep["first_node"][:],
                                  keep["ranges"][:].rearrange("p (c r) -> p c r", r=2)[:, :, 0])

        @block.gpsimd
        def _(pool):
            pool.dma_start(dst_chunks[:], io["dst_chunks"]).then_inc(chunks_in, 16)
            pool.dma_start(dst_int[:], io["dst"]).then_inc(dst_in, 16)
            for name in ("src", "y", "x"):
                pool.dma_start(keep[name][:], io[name]).then_inc(rest_in, 16)
            pool.wait_ge(zeros_made, 1)
            stores = 0
            for total in (keep["total0"], keep["total1"]):
                flat = total.rearrange("(p a) f -> p (a f)", p=P)
                for at in range(0, flat.shape[1], 3200):
                    pool.dma_start(flat[:, at:at + 3200], zeros[:]).then_inc(zeros_stored, 16)
                    stores += 1
            pool.wait_ge(ranges_made, 1)
            pool.dma_start(keep["range_table"].rearrange("a (p q) -> (a p) q", q=4),
                           range_rows[:].rearrange("p a b -> p (a b)")).then_inc(ranges_stored, 16)
            pool.wait_ge(ranges_stored, 16)
            pool.dma_start(keep["ranges"][:], keep["range_table"].broadcast_to([P, 2 * NCH])).then_inc(ranges_in, 16)
            pool.wait_ge(ranges_in, 16)
            pool.wait_ge(rest_in, 48)
            pool.wait_ge(zeros_stored, 16 * stores)


def sum_over_edges(nc, io, keep, layer):
    weighted = layer == 0
    table = keep["src_table"] if weighted else keep["x1_table"]
    total = keep["total0"] if weighted else keep["total1"]
    width = PROD if weighted else D
    with ExitStack() as ctx:
        def sb(name, shape, dt=F32):
            return ctx.enter_context(nc.sbuf_tensor(f"{name}{layer}", shape, dt))

        def sem(name):
            return ctx.enter_context(nc.semaphore(f"{name}{layer}"))

        def psum(name, shape):
            return ctx.enter_context(nc.psum_tensor(f"{name}{layer}", shape, F32))

        gathered = sb("gathered", [P, 2, CH, D])
        indices = sb("indices", [P, 2, CH], I32)
        spread = sb("spread", [P, CH, P])
        offset = sb("offset", [P, CH])
        slab = sb("slab", [P, D])
        window = psum("window", [P, 512])
        if weighted:
            product = sb("product", [P, 2, CH, PROD])
            radial = sb("radial", [RAD, 2, CHUNK])
            hidden = sb("hidden", [HID, CHUNK])
            hid_banks = psum("hid_banks", [HID, 2, 512])
            w_banks = psum("w_banks", [P, 4, 512])
        rows_of = product if weighted else gathered

        rows_in = [sem("rows_in_even"), sem("rows_in_odd")]
        indices_ready = sem("indices_ready")
        gathers_begun = sem("gathers_begun")
        radial_in = [sem("radial_in_even"), sem("radial_in_odd")]
        hid_ready = sem("hid_ready")
        hid_active = sem("hid_active")
        w_ready = sem("w_ready")
        w_used = sem("w_used")
        chunk_begun = sem("chunk_begun")
        spread_ready = sem("spread_ready")
        window_ready = sem("window_ready")
        window_added = sem("window_added")
        slab_in = sem("slab_in")
        slab_stored = sem("slab_stored")
        block = ctx.enter_context(nc.Block())
        banks_of = [list(range(b, min(b + 2, CH))) for b in range(0, CH, 2)]
        NB = len(banks_of)

        def bounds(eng, c):
            lo = eng.value_load(keep["ranges"][0:1, bass.ds(c * 2, 1)], min_val=0, max_val=NODES - 1)
            hi = eng.value_load(keep["ranges"][0:1, bass.ds(c * 2 + 1, 1)], min_val=0, max_val=NODES - 1)
            return lo, hi

        def stage_indices(copy, c, h):
            copy(indices[:, h, :], keep["src"][:, bass.ds(c * CH, CH)]).then_inc(indices_ready, 1)

        @block.gpsimd
        def _(pool):
            def gather(c, h):
                pool.wait_ge(indices_ready, c + 1)
                pool.sem_inc(gathers_begun, 1)
                for k in range(CH):
                    pool.indirect_dma_start(
                        gathered[:, h, k, :], None, table,
                        bass.IndirectOffsetOnAxis(indices[:, h, k:k + 1], axis=0),
                    ).then_inc(rows_in[h], 16)

            gather(0, 0)
            gather(1, 1)
            with pool.Fori(0, NCH // 2 - 1) as i:
                for h in range(2):
                    c = i * 2 + h
                    if weighted:
                        pool.wait_ge(w_used, (c + 1) * NB)
                    else:
                        pool.wait_ge(chunk_begun, c + 2)
                    gather(c + 2, h)

        @block.sync
        def _(sp):
            passes = sp.alloc_register(f"sp_passes{layer}")
            sp.reg_mov(passes, 0)
            with sp.Fori(0, NCH) as c:
                lo, hi = bounds(sp, c)
                with sp.Fori(lo, hi + 1, WIN) as base:
                    n = sp.snap(passes)
                    rows = total[bass.ds(base * NY, P), :]
                    sp.dma_start(slab[:], rows).then_inc(slab_in, 16)
                    sp.wait_ge(window_added, n + 2)
                    sp.dma_start(rows, slab[:]).then_inc(slab_stored, 16)
                    sp.wait_ge(slab_stored, n * 16 + 16)
                    sp.reg_add(passes, passes, 1)

        @block.tensor
        def _(pe):
            def make_hidden(c, h, i):
                pe.wait_ge(radial_in[h], i * 16 + 16)
                if not (isinstance(c, int) and c == 0):
                    pe.wait_ge(hid_active, c * 2)
                for q in range(2):
                    half = slice(q * CHUNK // 2, (q + 1) * CHUNK // 2)
                    pe.matmul(hid_banks[:, q, 0:CHUNK // 2], keep["fc1"][:], radial[:, h, half],
                              start=True, stop=True).then_inc(hid_ready, 1)

            def make_weights(c):
                for b, tiles in enumerate(banks_of):
                    if b < 2:
                        pe.wait_ge(hid_active, c * 2 + b + 1)
                    if not (isinstance(c, int) and c == 0):
                        pe.wait_ge(w_used, (c - 1) * NB + b + 1)
                    for j, k in enumerate(tiles):
                        mm = pe.matmul(w_banks[:, b, j * WNUM:(j + 1) * WNUM], hidden[:, k * P:(k + 1) * P],
                                       keep["fc2"][:], start=True, stop=True)
                    mm.then_inc(w_ready, 1)

            passes = pe.alloc_register(f"pe_passes{layer}")
            pe.reg_mov(passes, 0)

            def sum_windows(c, h, i):
                if not weighted:
                    pe.wait_ge(rows_in[h], (i + 1) * (16 * CH))
                lo, hi = bounds(pe, c)
                with pe.Fori(lo, hi + 1, WIN):
                    n = pe.snap(passes)
                    pe.wait_ge(window_added, n + 1)
                    for k in range(CH):
                        if k in (0, 2):
                            pe.wait_ge(spread_ready, n * 2 + (1 if k == 0 else 2))
                        mm = pe.matmul(window[:, 0:width], spread[:, k, :], rows_of[:, h, k, :],
                                       start=(k == 0), stop=(k == CH - 1))
                    mm.then_inc(window_ready, 1)
                    pe.reg_add(passes, passes, 1)

            if not weighted:
                with pe.Fori(0, NCH // 2) as i:
                    for h in range(2):
                        sum_windows(i * 2 + h, h, i)
                return
            make_hidden(0, 0, 0)
            make_weights(0)
            make_hidden(1, 1, 0)
            with pe.Fori(0, NCH // 2 - 1) as i:
                for h in range(2):
                    make_weights(i * 2 + h + 1)
                    make_hidden(i * 2 + h + 2, h, i + 1)
                    sum_windows(i * 2 + h, h, i)
            make_weights(NCH - 1)
            sum_windows(NCH - 2, 0, NCH // 2 - 1)
            sum_windows(NCH - 1, 1, NCH // 2 - 1)

        @block.scalar
        def _(act):
            if not weighted:
                stage_indices(nc.scalar.copy, 0, 0)
                stage_indices(nc.scalar.copy, 1, 1)
                with act.Fori(0, NCH // 2 - 1) as i:
                    for h in range(2):
                        act.wait_ge(rows_in[h], (i + 1) * (16 * CH))
                        stage_indices(nc.scalar.copy, i * 2 + h + 2, h)
                return

            def load_radial(c, h):
                act.dma_start(radial[:, h, :], io["radial_t"][:, bass.ds(c * CHUNK, CHUNK)]).then_inc(radial_in[h], 16)

            def activate(c):
                if not (isinstance(c, int) and c == 0):
                    act.wait_ge(w_ready, c * NB)
                for q in range(2):
                    act.wait_ge(hid_ready, c * 2 + q + 1)
                    nc.scalar.activation(hidden[:, q * CHUNK // 2:(q + 1) * CHUNK // 2],
                                         hid_banks[:, q, 0:CHUNK // 2], ACT.Silu,
                                         scale=float(1 / np.sqrt(RAD))).then_inc(hid_active, 1)

            load_radial(0, 0)
            load_radial(1, 1)
            activate(0)
            act.wait_ge(hid_ready, 2)
            load_radial(2, 0)
            with act.Fori(0, NCH // 2 - 2) as i:
                for h in range(2):
                    c = i * 2 + h + 1
                    activate(c)
                    load_radial(c + 2, (h + 1) % 2)
            activate(NCH - 3)
            load_radial(NCH - 1, 1)
            activate(NCH - 2)
            activate(NCH - 1)

        @block.vector
        def _(dve):
            passes = dve.alloc_register(f"dve_passes{layer}")
            dve.reg_mov(passes, 0)

            def weigh(c, h, i):
                dve.wait_ge(rows_in[h], (i + 1) * (16 * CH))
                stage_indices(nc.vector.tensor_copy, c + 2, h)
                for b, tiles in enumerate(banks_of):
                    m, k0 = len(tiles), tiles[0]
                    dve.wait_ge(w_ready, c * NB + b + 1)
                    w = w_banks[:, b, 0:m * WNUM].rearrange("p (t w) -> p t w", t=m)
                    nc.vector.tensor_tensor(
                        product[:, h, k0:k0 + m, :].rearrange("p t (a f) -> p t a f", a=2)[:, :, :, 0:MUL0],
                        w[:, :, 0:2 * MUL0].rearrange("p t (a f) -> p t a f", a=2),
                        gathered[:, h, k0:k0 + m, 0:MUL0].unsqueeze(2).broadcast_to([P, m, 2, MUL0]), ALU.mult)
                    for j, k in enumerate(tiles):
                        last = nc.vector.tensor_tensor(
                            product[:, h, k, :].rearrange("p (a f) -> p a f", a=2)[:, :, MUL0:D].rearrange(
                                "p a (c u) -> p a c u", c=3),
                            w[:, j, 2 * MUL0:].rearrange("p (a u) -> p a u", a=2).unsqueeze(2).broadcast_to(
                                [P, 2, 3, MUL1]),
                            gathered[:, h, k, MUL0:D].rearrange("p (c u) -> p c u", c=3).unsqueeze(1).broadcast_to(
                                [P, 2, 3, MUL1]), ALU.mult)
                    last.then_inc(w_used, 1)

            def make_spread(c):
                dve.drain()
                for k in range(CH):
                    ins = nc.vector.scalar_tensor_tensor(
                        spread[:, k, :].rearrange("p (n d) -> p n d", d=NY),
                        keep["node_of_column"][:].rearrange("p (n d) -> p n d", d=NY),
                        offset[:, k:k + 1],
                        keep["y"][:, bass.ds(c * CH + k, 1), :].broadcast_to([P, WIN, NY]),
                        ALU.is_equal, ALU.mult)
                    if k in (1, CH - 1):
                        ins.then_inc(spread_ready, 1)

            def add_window(n):
                dve.wait_ge(slab_in, n * 16 + 16)
                dve.wait_ge(window_ready, n + 1)
                if not weighted:
                    nc.vector.tensor_tensor(slab[:], window[:, 0:D], slab[:], ALU.add).then_inc(window_added, 1)
                else:
                    nc.vector.scalar_tensor_tensor(slab[:], window[:, 0:D], keep["harmonic_mask"][:, 0:1],
                                                   slab[:], ALU.mult, ALU.add)
                    dve.drain()
                    nc.vector.scalar_tensor_tensor(slab[:], window[:, D:PROD], keep["harmonic_mask"][:, 1:2],
                                                   slab[:], ALU.mult, ALU.add).then_inc(window_added, 1)
                dve.reg_add(passes, passes, 1)

            def sum_windows(c, between):
                lo, hi = bounds(dve, c)
                nc.vector.tensor_scalar(offset[:], keep["dst"][:, bass.ds(c * CH, CH)],
                                        keep["first_node"][:, bass.ds(c, 1)], None,
                                        ALU.subtract).then_inc(chunk_begun, 1)
                n = dve.snap(passes)
                make_spread(c)
                between()
                add_window(n)
                with dve.If(hi - lo >= WIN):
                    with dve.Fori(lo + WIN, hi + 1, WIN):
                        n = dve.snap(passes)
                        nc.vector.tensor_scalar(offset[:], offset[:], float(-WIN), None, ALU.add)
                        make_spread(c)
                        add_window(n)

            dve.sem_inc(window_added, 1)
            if weighted:
                stage_indices(nc.vector.tensor_copy, 0, 0)
                stage_indices(nc.vector.tensor_copy, 1, 1)
                weigh(0, 0, 0)
            with dve.Fori(0, NCH // 2 - 1) as i:
                for h in range(2):
                    c = i * 2 + h
                    sum_windows(c, lambda: weigh(c + 1, 1 - h, i + h) if weighted else None)
            last = NCH - 2
            sum_windows(last, lambda: weigh(last + 1, 1, NCH // 2 - 1) if weighted else None)
            sum_windows(last + 1, lambda: None)


def finish_nodes(nc, keep, layer, result):
    total = keep["total0"] if layer == 0 else keep["total1"]
    with ExitStack() as ctx:
        def sb(name, shape, dt=F32):
            return ctx.enter_context(nc.sbuf_tensor(f"{name}{layer}", shape, dt))

        def sem(name):
            return ctx.enter_context(nc.semaphore(f"{name}{layer}"))

        def psum(name, shape):
            return ctx.enter_context(nc.psum_tensor(f"{name}{layer}", shape, F32))

        x = keep["x"]
        if layer == 0:
            blocks = sb("blocks", [P, 2, G, NY, BLK])
            span = [MUL0 + MUL1] * 4
            width, outs = BLK, OUT0
        else:
            sums = sb("sums", [P, 2, G, NY, D])
            blocks = sb("blocks", [P, 2, G, NY, P])
            span = [MUL0 + MUL1] + [MUL0 + 2 * MUL1] * 3
            width, outs = P, D
            relus = sb("relus", [P, 2, G, D])
        turned = sb("turned", [P, 2, NY, P])
        small = sb("small", [P, 8, 2 * G])
        stats6 = sb("stats6", [P, G, 6])
        stats2 = sb("stats2", [P, G, 2])
        stats = sb("stats", [P, NT, 2])
        spreads = sb("spreads", [P, 3, NT])
        turn_banks = psum("turn_banks", [P, 2, 512])
        out_banks = psum("out_banks", [P, 2, 3 * 512])

        sums_in = [sem("sums_in_even"), sem("sums_in_odd")]
        copied = sem("copied")
        copies_begun = sem("copies_begun")
        combined = sem("combined")
        turned_in_psum = sem("turned_in_psum")
        turned_out = sem("turned_out")
        mapped = sem("mapped")
        group_read = sem("group_read")
        relus_made = sem("relus_made")
        angles_ready = sem("angles_ready")
        sines_ready = sem("sines_ready")
        var_ready = sem("var_ready")
        std_ready = sem("std_ready")
        shift_ready = sem("shift_ready")
        normed_dve = sem("normed_dve")
        normed_act = sem("normed_act")
        stored = sem("result_stored")
        block = ctx.enter_context(nc.Block())

        def slot(h, t):
            return out_banks[:, h, t * SLOT:t * SLOT + outs]

        @block.sync
        def _(sp):
            def load(g, h):
                for t in range(G):
                    if layer == 0:
                        sp.dma_start(blocks[:, h, t, :, MUL1:],
                                     total.rearrange("(t p d) f -> t p d f", p=P, d=NY)[bass.ds(g * G + t, 1)].rearrange(
                                         "t p d f -> p (t d) f")).then_inc(sums_in[h], 16)
                    else:
                        sp.dma_start(sums[:, h, t, :, :],
                                     total.rearrange("(t p d) f -> t p d f", p=P, d=NY)[bass.ds(g * G + t, 1)].rearrange(
                                         "t p d f -> p (t d) f")).then_inc(sums_in[h], 16)

            load(0, 0)
            load(1, 1)
            with sp.Fori(0, NG // 2 - 1) as i:
                for h in range(2):
                    g = i * 2 + h
                    if layer == 0:
                        sp.wait_ge(turned_in_psum, (g + 1) * G)
                    else:
                        sp.wait_ge(copied, g + 1)
                        sp.wait_ge(combined, g + 1)
                    load(g + 2, h)
            with sp.Fori(0, NG) as g:
                sp.wait_ge(normed_dve, g * (G - 2) + (G - 2))
                sp.wait_ge(normed_act, g * 2 + 2)
                sp.dma_start(result.rearrange("(t p) f -> p t f", p=P)[:, bass.ds(g * G, G), :],
                             x[:, bass.ds(g * G, G), :]).then_inc(stored, 16)
            sp.wait_ge(stored, 16 * NG)

        @block.gpsimd
        def _(pool):
            with pool.Fori(0, NG // 2) as i:
                for h in range(2):
                    g = i * 2 + h
                    pool.wait_ge(sums_in[h], (i + 1) * (16 * G))
                    if layer == 1:
                        pool.wait_ge(group_read, g + 1)
                    pool.sem_inc(copies_begun, 1)
                    if layer == 0:
                        nc.gpsimd.tensor_copy(
                            blocks[:, h, :, 1:, 0:MUL1],
                            blocks[:, h, :, 0, MUL1 + MUL0:].rearrange("p t (c u) -> p t c u", c=3)).then_inc(copied, 1)
                    else:
                        nc.gpsimd.tensor_copy(blocks[:, h, :, :, 0:MUL0], sums[:, h, :, :, 0:MUL0])
                        nc.gpsimd.tensor_copy(
                            blocks[:, h, :, 1:, MUL0:MUL0 + MUL1],
                            sums[:, h, :, 0, MUL0:].rearrange("p t (u c) -> p t c u", c=3)).then_inc(copied, 1)

        @block.tensor
        def _(pe):
            def turn(h, u, n):
                t = u % G
                pe.wait_ge(turned_out, n + 1)
                for d in range(NY):
                    mm = pe.transpose(turn_banks[0:span[d], u % 2, d * P:(d + 1) * P],
                                      blocks[:, h, t, d, 0:span[d]], keep["identity"][:])
                mm.then_inc(turned_in_psum, 1)

            def group_ready(g):
                pe.wait_ge(copied, g + 1)
                pe.wait_ge(combined, g + 1)

            with pe.Fori(0, NG // 2) as i:
                for u in range(2 * G):
                    h, t = divmod(u, G)
                    n = i * (2 * G) + u
                    if t == 0:
                        group_ready(i * 2 + h)
                        turn(h, u, n)
                    if t < G - 1:
                        turn(h, u + 1, n + 1)
                    if t == 0:
                        pe.wait_ge(group_read, i * 2 + h + 1)
                    pe.wait_ge(turned_out, n + 3)
                    out = slot(h, t)
                    first = outs - D
                    ws, wv = (keep["out_s"], keep["out_v"]) if layer == 0 else (keep["mix_s"], keep["mix_v"])
                    pe.matmul(out[:, 0:first + MUL0], turned[0:span[0], u % 2, 0, :], ws[:], start=True, stop=True)
                    for c in range(3):
                        mm = pe.matmul(out[:, first + MUL0:].rearrange("p (w c) -> p c w", c=3)[:, c, :],
                                       turned[0:span[1 + c], u % 2, 1 + c, :], wv[:], start=True, stop=True)
                    mm.then_inc(mapped, 1)

        @block.scalar
        def _(act):
            act.sem_inc(turned_out, 2)

            def make_relus(i, h):
                g = i * 2 + h
                act.wait_ge(mapped, (g + 1) * G + 2)
                act.wait_ge(group_read, g + 1)
                nc.scalar.activation(relus[:, h, :, :],
                                     out_banks[:, h, 0:G * SLOT].rearrange("p (t f) -> p t f", f=SLOT)[:, :, 0:D],
                                     ACT.Relu).then_inc(relus_made, 1)

            with act.Fori(0, NG // 2) as i:
                for u in range(2 * G):
                    h, t = divmod(u, G)
                    n = i * (2 * G) + u
                    act.wait_ge(turned_in_psum, n + 1)
                    act.wait_ge(mapped, n + 1)
                    if span[0] == span[1]:
                        nc.scalar.copy(turned[0:span[0], u % 2, :, :],
                                       turn_banks[0:span[0], u % 2, :].rearrange("p (d n) -> p d n", d=NY)
                                       ).then_inc(turned_out, 1)
                    else:
                        nc.scalar.copy(turned[0:span[0], u % 2, 0, :], turn_banks[0:span[0], u % 2, 0:P])
                        nc.scalar.copy(turned[0:span[1], u % 2, 1:, :],
                                       turn_banks[0:span[1], u % 2, P:].rearrange("p (d n) -> p d n", d=3)
                                       ).then_inc(turned_out, 1)
                    if layer == 1 and t == G - 1:
                        make_relus(i, h)
                    if layer == 0 and t == G - 1:
                        act.wait_ge(angles_ready, i * 2 + h + 1)
                        nc.scalar.activation(small[:, 6, :], small[:, 5, :], ACT.Sin).then_inc(sines_ready, 1)
            act.wait_ge(var_ready, 1)
            nc.scalar.activation(spreads[:, 1, :], spreads[:, 0, :], ACT.Sqrt).then_inc(std_ready, 1)
            act.wait_ge(shift_ready, 1)
            with act.Fori(0, NG) as g:
                for t in (G - 2, G - 1):
                    row = x[:, bass.ds(g * G + t, 1), :].rearrange("p t f -> p (t f)")
                    nc.scalar.activation(row, row, ACT.Identity, bias=spreads[:, 2, bass.ds(g * G + t, 1)],
                                         scale=spreads[:, 1, bass.ds(g * G + t, 1)]).then_inc(normed_act, 1)

        @block.vector
        def _(dve):
            dve.sem_inc(mapped, 2)
            dve.sem_inc(group_read, 2)
            vv = nc.vector

            def combine_blocks(i, h):
                dve.wait_ge(sums_in[h], (i + 1) * (16 * G))
                if layer == 0:
                    def part(c):
                        at = MUL1 + MUL0 + c * MUL1
                        return blocks[:, h, :, 1 + c, at:at + MUL1]
                    dve.wait_ge(copied, i * 2 + h + 1)
                    vv.tensor_tensor(blocks[:, h, :, 0, 0:MUL1], part(0), part(1), ALU.add)
                    dve.drain()
                    vv.tensor_tensor(blocks[:, h, :, 0, 0:MUL1], blocks[:, h, :, 0, 0:MUL1], part(2),
                                     ALU.add).then_inc(combined, 1)
                    return

                def moment(e, c):
                    return sums[:, h, :, 1 + e, MUL0:].rearrange("p t (u c) -> p t c u", c=3)[:, :, c, :]
                for c in range(3):
                    a, b = (c + 1) % 3, (c + 2) % 3
                    vv.tensor_tensor(blocks[:, h, :, 1 + c, MUL0 + MUL1:], moment(b, a), moment(a, b), ALU.subtract)
                dot = blocks[:, h, :, 0, MUL0:MUL0 + MUL1]
                vv.tensor_tensor(dot, moment(0, 0), moment(1, 1), ALU.add)
                dve.drain()
                vv.tensor_tensor(dot, dot, moment(2, 2), ALU.add).then_inc(combined, 1)

            def angles(g, h):
                attr = keep["attr"][:, bass.ds(g * G, G)]
                ang, turns, r, c = small[:, 0, 0:G], small[:, 1, 0:G], small[:, 5, 0:G], small[:, 5, G:]
                vv.tensor_tensor(ang, out_banks[:, h, 0:G * SLOT].rearrange("p (t f) -> p t f", f=SLOT)[:, :, 0],
                                 attr, ALU.mult)
                dve.drain()
                vv.tensor_scalar(turns, ang, float(1 / TURN), ROUND, ALU.mult, ALU.add)
                dve.drain()
                vv.tensor_scalar(turns, turns, -ROUND, None, ALU.add)
                dve.drain()
                vv.scalar_tensor_tensor(ang, turns, -TURN_HI, ang, ALU.mult, ALU.add)
                dve.drain()
                vv.scalar_tensor_tensor(ang, turns, -TURN_MID, ang, ALU.mult, ALU.add)
                dve.drain()
                vv.scalar_tensor_tensor(ang, turns, -TURN_LO, ang, ALU.mult, ALU.add)
                dve.drain()
                vv.tensor_scalar(small[:, 3, 0:G], ang, float(np.pi / 2), float(-TURN), ALU.is_gt, ALU.mult)
                vv.tensor_scalar(small[:, 4, 0:G], ang, float(np.pi / 2), None, ALU.add)
                vv.tensor_scalar(r, ang, PI_IN, -PI_IN, ALU.min, ALU.max)
                dve.drain()
                vv.tensor_tensor(c, small[:, 4, 0:G], small[:, 3, 0:G], ALU.add)
                dve.drain()
                vv.tensor_scalar(c, c, PI_IN, -PI_IN, ALU.min, ALU.max).then_inc(angles_ready, 1)
                dve.wait_ge(sines_ready, g + 1)
                vv.tensor_tensor(small[:, 7, 0:G], small[:, 6, 0:G], attr, ALU.mult)
                dve.drain()

            def finish_group(i, h):
                g = i * 2 + h
                dve.wait_ge(mapped, (g + 1) * G + 2)
                if layer == 0:
                    angles(g, h)
                for t in range(G):
                    if layer == 0:
                        row = x[:, bass.ds(g * G + t, 1), :].rearrange("p t f -> p (t f)")
                        vv.scalar_tensor_tensor(row, slot(h, t)[:, 1:], small[:, 7, t:t + 1], row,
                                                ALU.mult, ALU.add)
                if layer == 1:
                    dve.wait_ge(relus_made, g + 1)
                    rows = x[:, bass.ds(g * G, G), :].rearrange("p t f -> p (t f)")
                    vv.scalar_tensor_tensor(rows, rows, 2.0, relus[:, h, :, :].rearrange("p t f -> p (t f)"),
                                            ALU.mult, ALU.add)
                dve.drain().then_inc(group_read, 1)
                if layer == 0:
                    for t in range(G):
                        row = x[:, bass.ds(g * G + t, 1), :].rearrange("p t f -> p (t f)")
                        self_row = keep["sc"][:, bass.ds(g * G + t, 1), :].rearrange("p t f -> p (t f)")
                        vv.scalar_tensor_tensor(row, self_row, small[:, 6, G + t:G + t + 1], row,
                                                ALU.mult, ALU.add)
                    dve.drain()
                for t in range(G):
                    row = x[:, bass.ds(g * G + t, 1), :].rearrange("p t f -> p (t f)")
                    vv.bn_stats(stats6[:, t, :], row)
                dve.drain()
                for t in range(G):
                    vv.bn_aggr(stats2[:, t, :], stats6[:, t, :])
                dve.drain()
                vv.tensor_copy(stats[:, bass.ds(g * G, G), :], stats2[:])

            combine_blocks(0, 0)
            with dve.Fori(0, NG // 2 - 1) as i:
                combine_blocks(i, 1)
                finish_group(i, 0)
                combine_blocks(i + 1, 0)
                finish_group(i, 1)
            combine_blocks(NG // 2 - 1, 1)
            finish_group(NG // 2 - 1, 0)
            finish_group(NG // 2 - 1, 1)
            dve.drain()
            vv.tensor_scalar(spreads[:, 0, :], stats[:, :, 1], EPS, None, ALU.add).then_inc(var_ready, 1)
            dve.wait_ge(std_ready, 1)
            vv.reciprocal(spreads[:, 1, :], spreads[:, 1, :])
            dve.drain()
            vv.scalar_tensor_tensor(spreads[:, 2, :], stats[:, :, 0], -1.0, spreads[:, 1, :],
                                    ALU.mult, ALU.mult).then_inc(shift_ready, 1)
            dve.drain()
            with dve.Fori(0, NG) as g:
                for t in range(G - 2):
                    row = x[:, bass.ds(g * G + t, 1), :].rearrange("p t f -> p (t f)")
                    vv.tensor_scalar(row, row, spreads[:, 1, bass.ds(g * G + t, 1)],
                                     spreads[:, 2, bass.ds(g * G + t, 1)], ALU.mult, ALU.add).then_inc(normed_dve, 1)


def build(nc, io, out):
    with ExitStack() as ctx:
        def sb(name, shape, dt=F32):
            return ctx.enter_context(nc.sbuf_tensor(name, shape, dt))

        keep = {
            "x": sb("x_rows", [P, NT, D]),
            "sc": sb("self_rows", [P, NT, D]),
            "attr": sb("node_attr", [P, NT]),
            "src": sb("edge_src", [P, TILES + 2 * CH], I32),
            "dst": sb("edge_dst", [P, TILES]),
            "y": sb("edge_y", [P, TILES, NY]),
            "ranges": sb("ranges", [P, 2 * NCH], I32),
            "first_node": sb("first_node", [P, NCH]),
            "fc1": sb("fc1", [RAD, HID]),
            "fc2": sb("fc2", [HID, WNUM]),
            "out_s": sb("out_s", [MUL0 + MUL1, 1 + MUL0]),
            "out_v": sb("out_v", [MUL0 + MUL1, MUL1]),
            "mix_s": sb("mix_s", [MUL0 + MUL1, MUL0]),
            "mix_v": sb("mix_v", [MUL0 + 2 * MUL1, MUL1]),
            "node_of_column": sb("node_of_column", [P, P]),
            "identity": sb("identity", [P, P]),
            "harmonic_mask": sb("harmonic_mask", [P, 2]),
            "src_table": nc.dram_tensor("src_table", (NPAD, D), F32, kind="Internal").ap(),
            "x1_table": nc.dram_tensor("x1_table", (NPAD, D), F32, kind="Internal").ap(),
            "total0": nc.dram_tensor("total0", (NPAD * NY, D), F32, kind="Internal").ap(),
            "total1": nc.dram_tensor("total1", (NPAD * NY, D), F32, kind="Internal").ap(),
            "range_table": nc.dram_tensor("range_table", (1, 2 * NCH), I32, kind="Internal").ap(),
        }
        load_and_embed(nc, io, keep)
        sum_over_edges(nc, io, keep, 0)
        finish_nodes(nc, keep, 0, keep["x1_table"])
        sum_over_edges(nc, io, keep, 1)
        finish_nodes(nc, keep, 1, out)


def kernel(**inputs):
    import numpy as np
    import concourse.bacc as bacc
    from concourse.bass_utils import run_bass_kernel_spmd

    f = {name: np.asarray(a) for name, a in inputs.items()}

    def by_node(a):
        full = np.zeros((NPAD, a.shape[1]), a.dtype)
        full[:NODES] = a
        return np.ascontiguousarray(full.reshape(NT, P, -1).transpose(1, 0, 2))

    def by_edge(a, fill=0):
        full = np.full((EPAD, a.shape[1]), fill, a.dtype)
        full[:EDGES] = a
        return full

    def in_tiles(a):
        return np.ascontiguousarray(a.reshape(TILES, P, -1).transpose(1, 0, 2))

    x, y = f["x"], f["edge_attr_4"]
    x_t = np.zeros((D, NPAD), x.dtype)
    x_t[:MUL0, :NODES] = x[:, :MUL0].T
    x_t[MUL0:, :NODES] = x[:, MUL0:].reshape(NODES, MUL1, 3).transpose(2, 1, 0).reshape(3 * MUL1, NODES)
    dst = by_edge(f["dst"].astype(np.int32)[:, None], f["dst"][-1])
    arrays = {
        "x": by_node(x),
        "x_t": x_t,
        "attr": by_node(f["node_vec1"])[:, :, 0].copy(),
        "src": np.pad(in_tiles(by_edge(f["src"].astype(np.int32)[:, None]))[:, :, 0], ((0, 0), (0, 2 * CH))),
        "dst": in_tiles(dst)[:, :, 0].copy(),
        "dst_chunks": dst.reshape(NCH // 2, 2, CHUNK),
        "y": in_tiles(by_edge(y)),
        "radial_t": np.ascontiguousarray(by_edge(f["edge_attr_8"]).T),
        "mix_s_t": np.concatenate([f["L1_gnn_W1"].T, f["L1_gnn_W2"].T], axis=1),
        "mix_v_t": np.concatenate([f["L1_gnn_W3"].T, f["L1_gnn_W4"].T, f["L1_gnn_W5"].T], axis=1),
        "node_of_column": np.broadcast_to(np.arange(P, dtype=np.float32) // NY, (P, P)).copy(),
        "identity": np.eye(P, dtype=np.float32),
        "harmonic_mask": np.stack([np.arange(P) % NY == 0, np.arange(P) % NY != 0], axis=1).astype(np.float32),
    }
    for name in ("L0_gnn_W_sc_s", "L0_gnn_W_sc_v", "L0_gnn_W1_s", "L0_gnn_W1_v", "L0_gnn_W2_s", "L0_gnn_W2_v",
                 "L0_gnn_W3", "L0_gnn_fcW1", "L0_gnn_fcW2", "L1_gnn_Ws", "L1_gnn_Wv"):
        arrays[name] = np.ascontiguousarray(f[name])

    nc = bacc.Bacc("TRN2", target_bir_lowering=False, num_devices=1)
    io = {name: nc.dram_tensor(f"in_{name}", a.shape, mybir.dt.from_np(a.dtype), kind="ExternalInput").ap()
          for name, a in arrays.items()}
    out = nc.dram_tensor("out_rows", (NPAD, D), F32, kind="ExternalOutput").ap()
    build(nc, io, out)
    run = run_bass_kernel_spmd(nc, [{f"in_{name}": a for name, a in arrays.items()}], core_ids=[0])
    return run.results[0]["out_rows"][:NODES]
```

```python
from contextlib import ExitStack

import numpy as np

import concourse.bass as bass
from concourse import mybir

ALU = mybir.AluOpType
ACT = mybir.ActivationFunctionType
F32 = mybir.dt.float32
I32 = mybir.dt.int32
AX = mybir.AxisListType

P = 128
NODES, EDGES = 6250, 200000
MUL0, MUL1 = 64, 32
D = MUL0 + 3 * MUL1
NY = 4
RAD, HID = 8, 64
WNUM = 2 * MUL0 + 2 * MUL1

CH = 7
CHUNK = CH * P
NCH = -(-EDGES // CHUNK)
RING = 4
assert NCH % RING == 0
TILES = NCH * CH
EPAD = TILES * P
WIN = P // NY
FRONT = (CH + 1) // 2
SPAN = FRONT * P

G = 5
NG = 10
NT = G * NG
NPAD = NT * P
assert NPAD >= NODES + WIN

PROD = 2 * D
BLK = MUL1 + D
OUT0 = 1 + D
SLOT = 256

INV3, INV6 = 1 / np.sqrt(3.0), 1 / np.sqrt(6.0)
MIX = 1 / np.sqrt(MUL0 + MUL1)
C1 = np.sqrt(3.0 / (MUL0 + 2 * MUL1))
LIN_S, LIN_V = 1 / np.sqrt(MUL0), 1 / np.sqrt(MUL1)
NEIGHBORS = 10.0
EPS = 1e-5

TURN = 2 * np.pi
TURN_HI = 6.28125
TURN_MID = float(np.float32(TURN - TURN_HI))
TURN_LO = float(TURN - TURN_HI - TURN_MID)
ROUND = 1.5 * 2.0**23
PI_IN = 3.1415925


def load_and_embed(nc, io, keep):
    with ExitStack() as ctx:
        def sb(name, shape, dt=F32):
            return ctx.enter_context(nc.sbuf_tensor(name, shape, dt))

        def sem(name):
            return ctx.enter_context(nc.semaphore(name))

        xs_t = sb("xs_t", [MUL0, 2, G * P])
        xv_t = sb("xv_t", [MUL1, 2, 3, G * P])
        node_ws = sb("node_ws", [MUL0, 2 * MUL0])
        node_wv = sb("node_wv", [MUL1, 2 * MUL1])
        pre_s = sb("pre_s", [MUL0, MUL0 + MUL1 + MUL0])
        pre_v = sb("pre_v", [MUL1, MUL0 + 2 * MUL1 + MUL1])
        src_rows = sb("src_rows", [P, NT, D])
        zeros = sb("zeros", [P, 3200])
        dst_int = sb("dst_int", [P, TILES], I32)
        dst_chunks = sb("dst_chunks", [NCH // 2, 2, CHUNK], I32)
        range_rows = sb("range_rows", [NCH // 2, 2, 2], I32)
        banks = ctx.enter_context(nc.psum_tensor("embed_banks", [P, G, 512], F32))
        pre_bank = ctx.enter_context(nc.psum_tensor("pre_bank", [P, 2, 512], F32))

        weights_in = sem("weights_in")
        weights_scaled = sem("weights_scaled")
        fc1_cleared = sem("fc1_cleared")
        attr_in = sem("attr_in")
        xt_in = [sem("xt_in0"), sem("xt_in1")]
        embedded = sem("embedded")
        rows_out = sem("rows_out")
        self_out = sem("self_out")
        rows_stored = sem("rows_stored")
        zeros_made = sem("zeros_made")
        zeros_stored = sem("zeros_stored")
        chunks_in = sem("chunks_in")
        ranges_made = sem("ranges_made")
        ranges_stored = sem("ranges_stored")
        ranges_in = sem("ranges_in")
        dst_in = sem("dst_in")
        rest_in = sem("rest_in")
        premul = sem("premul")
        N_WEIGHTS = 4 + 4 + 6 + 4 + 3
        block = ctx.enter_context(nc.Block())

        @block.sync
        def _(sp):
            def load_columns(g, h):
                cols = bass.ds(g * (G * P), G * P)
                sp.dma_start(xs_t[:, h, :], io["x_t"][0:MUL0, cols]).then_inc(xt_in[h], 16)
                sp.dma_start(xv_t[:, h, :, :],
                             io["x_t"][MUL0:D, :].rearrange("(i u) n -> u i n", i=3)[:, :, cols]
                             ).then_inc(xt_in[h], 16)

            for dst, src in (
                (node_ws[:, 0:MUL0], io["L0_gnn_W1_s"]), (node_ws[:, MUL0:], io["L0_gnn_W_sc_s"]),
                (node_wv[:, 0:MUL1], io["L0_gnn_W1_v"]), (node_wv[:, MUL1:], io["L0_gnn_W_sc_v"]),
            ):
                sp.dma_start(dst, src).then_inc(weights_in, 16)
            load_columns(0, 0)
            load_columns(1, 1)
            sp.wait_ge(fc1_cleared, 1)
            sp.dma_start(keep["attr"][:], io["attr"]).then_inc(attr_in, 16)
            rest_s, rest_v = MUL0, MUL0
            for dst, src in (
                (keep["fc1"][0:RAD, 0:HID], io["L0_gnn_fcW1"]), (keep["fc1"][RAD:, HID:], io["L0_gnn_fcW1"]),
                (keep["fc2"][0:HID, :], io["L0_gnn_fcW2"]), (keep["fc2"][HID:, :], io["L0_gnn_fcW2"]),
                (keep["out_s"][0:MUL1, 1:], io["L0_gnn_W2_s"][rest_s:, :]),
                (keep["out_s"][MUL1:, 1:], io["L0_gnn_W2_s"][0:MUL0, :]),
                (keep["out_s"][0:MUL1, 0:1], io["L0_gnn_W3"][rest_s:, :]),
                (keep["out_s"][MUL1:, 0:1], io["L0_gnn_W3"][0:MUL0, :]),
                (keep["out_v"][0:MUL1, :], io["L0_gnn_W2_v"][rest_v:, :]),
                (keep["out_v"][MUL1:, :], io["L0_gnn_W2_v"][0:MUL0, :]),
                (pre_s[:, 0:MUL0 + MUL1], io["mix_s_t"]), (pre_s[:, MUL0 + MUL1:], io["L1_gnn_Ws"]),
                (pre_v[:, 0:MUL0 + 2 * MUL1], io["mix_v_t"]), (pre_v[:, MUL0 + 2 * MUL1:], io["L1_gnn_Wv"]),
                (keep["node_of_column"][:], io["node_of_column"]), (keep["identity"][:], io["identity"]),
                (keep["harmonic_mask"][:], io["harmonic_mask"]),
            ):
                sp.dma_start(dst, src).then_inc(weights_in, 16)

            def store_rows(g):
                sp.wait_ge(rows_out, (g + 1) * G)
                sp.dma_start(keep["src_table"].rearrange("(t p) f -> p t f", p=P)[:, bass.ds(g * G, G), :],
                             src_rows[:, bass.ds(g * G, G), :]).then_inc(rows_stored, 16)

            with sp.Fori(0, NG // 2 - 1) as i:
                for h in range(2):
                    store_rows(i * 2 + h)
                    sp.wait_ge(embedded, (i * 2 + h + 1) * G)
                    load_columns(i * 2 + h + 2, h)
            for g in (NG - 2, NG - 1):
                store_rows(g)
            sp.wait_ge(rows_stored, 16 * NG)

        @block.tensor
        def _(pe):
            pe.wait_ge(weights_scaled, 2)
            with pe.Fori(0, NG // 2) as i:
                for h in range(2):
                    pe.wait_ge(xt_in[h], i * 32 + 32)
                    for t in range(G):
                        n = (i * 2 + h) * G + t
                        pe.wait_ge(self_out, n + 1)
                        cols = slice(t * P, t * P + P)
                        pe.matmul(banks[:, t, 0:2 * MUL0], xs_t[:, h, cols], node_ws[:], start=True, stop=True)
                        for c in range(3):
                            at = 2 * MUL0 + c * 2 * MUL1
                            mm = pe.matmul(banks[:, t, at:at + 2 * MUL1], xv_t[:, h, c, cols], node_wv[:],
                                           start=True, stop=True)
                        mm.then_inc(embedded, 1)
            pe.wait_ge(weights_in, 16 * N_WEIGHTS)
            pe.matmul(pre_bank[0:MUL0 + MUL1, 0, 0:MUL0], pre_s[:, 0:MUL0 + MUL1], pre_s[:, MUL0 + MUL1:],
                      start=True, stop=True)
            pe.matmul(pre_bank[:, 1, 0:MUL1], pre_v[:, 0:MUL0 + 2 * MUL1], pre_v[:, MUL0 + 2 * MUL1:],
                      start=True, stop=True).then_inc(premul, 1)

        @block.scalar
        def _(act):
            act.wait_ge(attr_in, 16)
            with act.Fori(0, NG) as g:
                for t in range(G):
                    n = g * G + t
                    act.wait_ge(embedded, n + 1)
                    scale = keep["attr"][:, bass.ds(n, 1)]
                    nc.scalar.activation(src_rows[:, bass.ds(n, 1), 0:MUL0].rearrange("p t f -> p (t f)"),
                                         banks[:, t, 0:MUL0], ACT.Copy, scale=scale)
                    nc.scalar.activation(
                        src_rows[:, bass.ds(n, 1), MUL0:].rearrange("p t (c f) -> p (t c) f", c=3),
                        banks[:, t, 2 * MUL0:2 * MUL0 + 6 * MUL1].rearrange("p (c f) -> p c f", c=3)[:, :, 0:MUL1],
                        ACT.Copy, scale=scale).then_inc(rows_out, 1)

        @block.vector
        def _(dve):
            nc.vector.memset(keep["fc1"][:], 0.0).then_inc(fc1_cleared, 1)
            nc.vector.memset(zeros[:], 0.0).then_inc(zeros_made, 1)
            dve.sem_inc(self_out, G)
            dve.wait_ge(weights_in, 16 * N_WEIGHTS)
            nc.vector.tensor_scalar(node_ws[:], node_ws[:], float(LIN_S), None, ALU.mult).then_inc(weights_scaled, 1)
            nc.vector.tensor_scalar(node_wv[:], node_wv[:], float(LIN_V), None, ALU.mult).then_inc(weights_scaled, 1)
            nc.vector.tensor_scalar(keep["fc2"][:], keep["fc2"][:], float(1 / np.sqrt(HID)), None, ALU.mult)
            out_scale = float(MIX / np.sqrt(NEIGHBORS))
            nc.vector.tensor_scalar(keep["out_v"][:], keep["out_v"][:], out_scale, None, ALU.mult)
            nc.vector.tensor_scalar(keep["out_s"][:], keep["out_s"][:], out_scale, None, ALU.mult)
            dve.drain()
            nc.vector.tensor_scalar(keep["out_s"][0:MUL1, :], keep["out_s"][0:MUL1, :], float(INV3), None, ALU.mult)
            dve.drain()
            nc.vector.tensor_scalar(keep["out_s"][:, 0:1], keep["out_s"][:, 0:1], 0.1, None, ALU.mult)
            dve.wait_ge(attr_in, 16)
            with dve.Fori(0, NG) as g:
                for t in range(G):
                    n = g * G + t
                    dve.wait_ge(embedded, n + 1)
                    dve.wait_ge(rows_out, n + 1)
                    scale = keep["attr"][:, bass.ds(n, 1)]
                    row = keep["sc"][:, bass.ds(n, 1), :].rearrange("p t f -> p (t f)")
                    nc.vector.tensor_scalar(row[:, 0:MUL0], banks[:, t, MUL0:2 * MUL0], scale, None, ALU.mult)
                    nc.vector.tensor_scalar(
                        row[:, MUL0:].rearrange("p (w c) -> p c w", c=3),
                        banks[:, t, 2 * MUL0:2 * MUL0 + 6 * MUL1].rearrange("p (c f) -> p c f", c=3)[:, :, MUL1:],
                        scale, None, ALU.mult).then_inc(self_out, 1)
            dve.wait_ge(chunks_in, 16)
            nc.vector.tensor_reduce(range_rows[:, :, 0], dst_chunks[:], AX.X, ALU.min)
            nc.vector.tensor_reduce(range_rows[:, :, 1], dst_chunks[:], AX.X, ALU.max).then_inc(ranges_made, 1)
            dve.wait_ge(dst_in, 16)
            nc.vector.tensor_copy(keep["dst"][:], dst_int[:])
            dve.wait_ge(premul, 1)
            nc.vector.tensor_scalar(keep["mix_s"][:], pre_bank[0:MUL0 + MUL1, 0, 0:MUL0],
                                    float(MIX * LIN_S), None, ALU.mult)
            nc.vector.tensor_scalar(keep["mix_v"][:], pre_bank[:, 1, 0:MUL1],
                                    float(C1 * INV3 * LIN_V), None, ALU.mult)
            dve.drain()
            nc.vector.tensor_scalar(keep["mix_s"][MUL0:, :], keep["mix_s"][MUL0:, :], float(INV3), None, ALU.mult)
            nc.vector.tensor_scalar(keep["mix_v"][MUL0 + MUL1:, :], keep["mix_v"][MUL0 + MUL1:, :],
                                    float(INV6 / INV3), None, ALU.mult)
            dve.wait_ge(ranges_in, 16)
            nc.vector.tensor_copy(keep["first_node"][:],
                                  keep["ranges"][:].rearrange("p (c r) -> p c r", r=2)[:, :, 0])

        @block.gpsimd
        def _(pool):
            pool.dma_start(dst_chunks[:], io["dst_chunks"]).then_inc(chunks_in, 16)
            pool.dma_start(dst_int[:], io["dst"]).then_inc(dst_in, 16)
            for name in ("src", "y", "x"):
                pool.dma_start(keep[name][:], io[name]).then_inc(rest_in, 16)
            pool.wait_ge(zeros_made, 1)
            stores = 0
            for total in (keep["total0"], keep["total1"]):
                flat = total.rearrange("(p a) f -> p (a f)", p=P)
                for at in range(0, flat.shape[1], 3200):
                    pool.dma_start(flat[:, at:at + 3200], zeros[:]).then_inc(zeros_stored, 16)
                    stores += 1
            pool.wait_ge(ranges_made, 1)
            pool.dma_start(keep["range_table"].rearrange("a (p q) -> (a p) q", q=4),
                           range_rows[:].rearrange("p a b -> p (a b)")).then_inc(ranges_stored, 16)
            pool.wait_ge(ranges_stored, 16)
            pool.dma_start(keep["ranges"][:], keep["range_table"].broadcast_to([P, 2 * NCH])).then_inc(ranges_in, 16)
            pool.wait_ge(ranges_in, 16)
            pool.wait_ge(rest_in, 48)
            pool.wait_ge(zeros_stored, 16 * stores)


def sum_over_edges(nc, io, keep, layer):
    weighted = layer == 0
    table = keep["src_table"] if weighted else keep["x1_table"]
    total = keep["total0"] if weighted else keep["total1"]
    width = PROD if weighted else D
    with ExitStack() as ctx:
        def sb(name, shape, dt=F32):
            return ctx.enter_context(nc.sbuf_tensor(f"{name}{layer}", shape, dt))

        def sem(name):
            return ctx.enter_context(nc.semaphore(f"{name}{layer}"))

        def psum(name, shape):
            return ctx.enter_context(nc.psum_tensor(f"{name}{layer}", shape, F32))

        gathered = sb("gathered", [P, RING, CH, D])
        indices = sb("indices", [P, RING, CH], I32)
        spread = sb("spread", [P, CH, P])
        offset = sb("offset", [P, CH])
        slab = sb("slab", [P, D])
        window = psum("window", [P, 512])
        if weighted:
            product = sb("product", [P, 2, CH, PROD])
            radial = sb("radial", [2 * RAD, 2, SPAN])
            hidden = sb("hidden", [2 * HID, SPAN])
            hid_bank = psum("hid_bank", [2 * HID, 512])
            w_banks = psum("w_banks", [P, 4, 512])

        rows_in = [sem(f"rows_in_slot{q}_") for q in range(RING)]
        indices_ready = sem("indices_ready")
        gathers_begun = sem("gathers_begun")
        radial_in = [sem("radial_in_even"), sem("radial_in_odd")]
        pad_cleared = sem("pad_cleared")
        hid_ready = sem("hid_ready")
        hid_active = sem("hid_active")
        w_ready = sem("w_ready")
        w_used = sem("w_used")
        chunk_begun = sem("chunk_begun")
        spread_ready = sem("spread_ready")
        window_ready = sem("window_ready")
        window_added = sem("window_added")
        slab_in = sem("slab_in")
        slab_stored = sem("slab_stored")
        all_stored = sem("all_stored")
        block = ctx.enter_context(nc.Block())
        banks_of = [[0, 1], [4, 5], [6], [2, 3]]
        NB = len(banks_of)

        def over_chunks(eng, step):
            with eng.Fori(0, NCH // RING - 1) as i:
                for h in range(RING):
                    step(i * RING + h, i, h)
            for h in range(RING):
                step(NCH - RING + h, NCH // RING - 1, h)

        def is_last(c, ahead):
            return isinstance(c, int) and c + ahead >= NCH

        def lap(i, h, ring):
            return i * (RING // ring) + (h // ring + 1)

        def bounds(eng, c, addressed=False):
            known = dict(min_val=0, max_val=NODES - 1) if addressed else {}
            lo = eng.value_load(keep["ranges"][0:1, bass.ds(c * 2, 1)], **known)
            hi = eng.value_load(keep["ranges"][0:1, bass.ds(c * 2 + 1, 1)], **known)
            return lo, hi

        def stage_indices(copy, c, h):
            copy(indices[:, h, :], keep["src"][:, bass.ds(c * CH, CH)]).then_inc(indices_ready, 1)

        @block.gpsimd
        def _(pool):
            def gather(c, h):
                pool.wait_ge(indices_ready, c + 1)
                pool.sem_inc(gathers_begun, 1)
                for k in range(CH):
                    pool.indirect_dma_start(
                        gathered[:, h, k, :], None, table,
                        bass.IndirectOffsetOnAxis(indices[:, h, k:k + 1], axis=0),
                    ).then_inc(rows_in[h], 16)

            for c in range(RING):
                gather(c, c)

            def gather_ahead(c, i, h):
                if is_last(c, RING):
                    return
                if weighted:
                    pool.wait_ge(w_used, (c + 1) * NB)
                else:
                    pool.wait_ge(chunk_begun, c + 2)
                gather(c + RING, h)

            over_chunks(pool, gather_ahead)

        @block.sync
        def _(sp):
            passes = sp.alloc_register(f"sp_passes{layer}")
            sp.reg_mov(passes, 0)
            sp.dma_start(slab[:], total[0:P, :]).then_inc(slab_stored, 16)
            with sp.Fori(0, NCH) as c:
                lo, hi = bounds(sp, c, addressed=True)
                with sp.Fori(lo, hi + 1, WIN) as base:
                    n = sp.snap(passes)
                    rows = total[bass.ds(base * NY, P), :]
                    sp.wait_ge(slab_stored, n * 16 + 16)
                    sp.dma_start(slab[:], rows).then_inc(slab_in, 16)
                    sp.wait_ge(window_added, n + 2)
                    sp.dma_start(rows, slab[:]).then_inc(slab_stored, 16)
                    sp.reg_add(passes, passes, 1)
            n = sp.snap(passes)
            sp.wait_ge(slab_stored, n * 16 + 16)
            sp.sem_inc(all_stored, 1)

        @block.tensor
        def _(pe):
            def make_hidden(c, i, h):
                pe.wait_ge(radial_in[h % 2], lap(i, h, 2) * 32)
                if not (isinstance(c, int) and c == 0):
                    pe.wait_ge(hid_active, c)
                pe.matmul(hid_bank[:, 0:SPAN], keep["fc1"][:], radial[:, h % 2, :],
                          start=True, stop=True).then_inc(hid_ready, 1)

            def make_weights(c):
                pe.wait_ge(hid_active, c + 1)
                for banks, tiles in (((0, 1), (0, 4, 1, 5)), ((2, 3), (6, 2, 3))):
                    if not (isinstance(c, int) and c == 0):
                        pe.wait_ge(w_used, (c - 1) * NB + (banks[1] + 1))
                    for k in tiles:
                        b = next(b for b in banks if k in banks_of[b])
                        j = banks_of[b].index(k)
                        part = slice(0, HID) if k < FRONT else slice(HID, 2 * HID)
                        at = k % FRONT * P
                        mm = pe.matmul(w_banks[:, b, j * WNUM:(j + 1) * WNUM], hidden[part, at:at + P],
                                       keep["fc2"][part, :], start=True, stop=True)
                        if k == banks_of[b][-1]:
                            mm.then_inc(w_ready, 1)

            passes = pe.alloc_register(f"pe_passes{layer}")
            pe.reg_mov(passes, 0)

            def sum_windows(c, i, h):
                if not weighted:
                    pe.wait_ge(rows_in[h], lap(i, h, RING) * (16 * CH))
                lo, hi = bounds(pe, c)
                with pe.Fori(lo, hi + 1, WIN):
                    n = pe.snap(passes)
                    pe.wait_ge(window_added, n + 1)
                    for k in range(CH):
                        if k in (0, 2):
                            pe.wait_ge(spread_ready, n * 2 + (1 if k == 0 else 2))
                        mm = pe.matmul(window[:, 0:width], spread[:, k, :],
                                       product[:, h % 2, k, :] if weighted else gathered[:, h, k, :],
                                       start=(k == 0), stop=(k == CH - 1))
                    mm.then_inc(window_ready, 1)
                    pe.reg_add(passes, passes, 1)

            if weighted:
                make_hidden(0, 0, 0)
                make_weights(0)
                make_hidden(1, 0, 1)

            def step(c, i, h):
                if weighted and not is_last(c, 1):
                    make_weights(c + 1)
                if weighted and not is_last(c, 2):
                    make_hidden(c + 2, i, h + 2)
                sum_windows(c, i, h)

            over_chunks(pe, step)

        @block.scalar
        def _(act):
            if not weighted:
                for c in range(RING):
                    stage_indices(nc.scalar.copy, c, c)

                def stage_ahead(c, i, h):
                    if not is_last(c, RING):
                        act.wait_ge(rows_in[h], lap(i, h, RING) * (16 * CH))
                        stage_indices(nc.scalar.copy, c + RING, h)

                over_chunks(act, stage_ahead)
                return

            def load_radial(c, h):
                for rows, at, n in ((slice(0, RAD), 0, SPAN), (slice(RAD, 2 * RAD), SPAN, CHUNK - SPAN)):
                    act.dma_start(radial[rows, h % 2, 0:n],
                                  io["radial_t"][:, bass.ds(c * CHUNK + at, n)]).then_inc(radial_in[h % 2], 16)

            act.wait_ge(pad_cleared, 1)
            load_radial(0, 0)
            load_radial(1, 1)

            def activate(c, i, h):
                if not (isinstance(c, int) and c == 0):
                    act.wait_ge(w_ready, c * NB)
                act.wait_ge(hid_ready, c + 1)
                nc.scalar.activation(hidden[:], hid_bank[:, 0:SPAN], ACT.Silu,
                                     scale=float(1 / np.sqrt(RAD))).then_inc(hid_active, 1)
                if not is_last(c, 2):
                    load_radial(c + 2, h)

            activate(0, 0, 0)
            with act.Fori(0, NCH // RING - 1) as i:
                for h in range(1, RING + 1):
                    activate(i * RING + h, i, h)
            for h in range(1, RING):
                activate(NCH - RING + h, NCH // RING - 1, h)

        @block.vector
        def _(dve):
            passes = dve.alloc_register(f"dve_passes{layer}")
            dve.reg_mov(passes, 0)

            def weigh(c, i, h):
                slot, half = h % RING, h % 2
                dve.wait_ge(rows_in[slot], lap(i, h, RING) * (16 * CH))
                if not is_last(c, RING):
                    stage_indices(nc.vector.tensor_copy, c + RING, slot)
                for b, tiles in enumerate(banks_of):
                    m, pair = len(tiles), slice(tiles[0], tiles[-1] + 1)
                    dve.wait_ge(w_ready, c * NB + b + 1)
                    w = w_banks[:, b, 0:m * WNUM].rearrange("p (t w) -> p t w", t=m)
                    nc.vector.tensor_tensor(
                        product[:, half, pair, :].rearrange("p t (a f) -> p t a f", a=2)[:, :, :, 0:MUL0],
                        w[:, :, 0:2 * MUL0].rearrange("p t (a f) -> p t a f", a=2),
                        gathered[:, slot, pair, 0:MUL0].unsqueeze(2).broadcast_to([P, m, 2, MUL0]), ALU.mult)
                    for j, k in enumerate(tiles):
                        last = nc.vector.tensor_tensor(
                            product[:, half, k, :].rearrange("p (a f) -> p a f", a=2)[:, :, MUL0:D].rearrange(
                                "p a (c u) -> p a c u", c=3),
                            w[:, j, 2 * MUL0:].rearrange("p (a u) -> p a u", a=2).unsqueeze(2).broadcast_to(
                                [P, 2, 3, MUL1]),
                            gathered[:, slot, k, MUL0:D].rearrange("p (c u) -> p c u", c=3).unsqueeze(1).broadcast_to(
                                [P, 2, 3, MUL1]), ALU.mult)
                    last.then_inc(w_used, 1)

            def make_spread(c):
                dve.drain()
                for k in range(CH):
                    ins = nc.vector.scalar_tensor_tensor(
                        spread[:, k, :].rearrange("p (n d) -> p n d", d=NY),
                        keep["node_of_column"][:].rearrange("p (n d) -> p n d", d=NY),
                        offset[:, k:k + 1],
                        keep["y"][:, bass.ds(c * CH + k, 1), :].broadcast_to([P, WIN, NY]),
                        ALU.is_equal, ALU.mult)
                    if k in (1, CH - 1):
                        ins.then_inc(spread_ready, 1)

            def add_window(n):
                dve.wait_ge(slab_in, n * 16 + 16)
                dve.wait_ge(window_ready, n + 1)
                if not weighted:
                    nc.vector.tensor_tensor(slab[:], window[:, 0:D], slab[:], ALU.add).then_inc(window_added, 1)
                else:
                    nc.vector.scalar_tensor_tensor(slab[:], window[:, 0:D], keep["harmonic_mask"][:, 0:1],
                                                   slab[:], ALU.mult, ALU.add)
                    dve.drain()
                    nc.vector.scalar_tensor_tensor(slab[:], window[:, D:PROD], keep["harmonic_mask"][:, 1:2],
                                                   slab[:], ALU.mult, ALU.add).then_inc(window_added, 1)
                dve.reg_add(passes, passes, 1)

            def sum_windows(c, between):
                lo, hi = bounds(dve, c)
                nc.vector.tensor_scalar(offset[:], keep["dst"][:, bass.ds(c * CH, CH)],
                                        keep["first_node"][:, bass.ds(c, 1)], None,
                                        ALU.subtract).then_inc(chunk_begun, 1)
                n = dve.snap(passes)
                make_spread(c)
                between()
                add_window(n)
                with dve.If(hi - lo >= WIN):
                    with dve.Fori(lo + WIN, hi + 1, WIN):
                        n = dve.snap(passes)
                        nc.vector.tensor_scalar(offset[:], offset[:], float(-WIN), None, ALU.add)
                        make_spread(c)
                        add_window(n)

            dve.sem_inc(window_added, 1)
            if weighted:
                nc.vector.memset(radial[:, :, CHUNK - SPAN:], 0.0)
                dve.drain().then_inc(pad_cleared, 1)
                for c in range(RING):
                    stage_indices(nc.vector.tensor_copy, c, c)
                weigh(0, 0, 0)

            def step(c, i, h):
                if weighted and not is_last(c, 1):
                    sum_windows(c, lambda: weigh(c + 1, i, h + 1))
                else:
                    sum_windows(c, lambda: None)

            over_chunks(dve, step)


def finish_nodes(nc, keep, layer, result):
    total = keep["total0"] if layer == 0 else keep["total1"]
    with ExitStack() as ctx:
        def sb(name, shape, dt=F32):
            return ctx.enter_context(nc.sbuf_tensor(f"{name}{layer}", shape, dt))

        def sem(name):
            return ctx.enter_context(nc.semaphore(f"{name}{layer}"))

        def psum(name, shape):
            return ctx.enter_context(nc.psum_tensor(f"{name}{layer}", shape, F32))

        x = keep["x"]
        if layer == 0:
            blocks = sb("blocks", [P, 2, G, NY, BLK])
            span = [MUL0 + MUL1] * 4
            width, outs = BLK, OUT0
        else:
            sums = sb("sums", [P, 2, G, NY, D])
            blocks = sb("blocks", [P, 2, G, NY, P])
            span = [MUL0 + MUL1] + [MUL0 + 2 * MUL1] * 3
            width, outs = P, D
            relus = sb("relus", [P, 2, G, D])
        turned = sb("turned", [P, 2, NY, P])
        small = sb("small", [P, 8, 2 * G])
        stats6 = sb("stats6", [P, G, 6])
        stats2 = sb("stats2", [P, G, 2])
        stats = sb("stats", [P, NT, 2])
        spreads = sb("spreads", [P, 3, NT])
        turn_banks = psum("turn_banks", [P, 2, 512])
        out_banks = psum("out_banks", [P, 2, 3 * 512])

        sums_in = [sem("sums_in_even"), sem("sums_in_odd")]
        copied = sem("copied")
        copies_begun = sem("copies_begun")
        combined = sem("combined")
        turned_in_psum = sem("turned_in_psum")
        turned_out = sem("turned_out")
        mapped = sem("mapped")
        group_read = sem("group_read")
        relus_made = sem("relus_made")
        angles_ready = sem("angles_ready")
        sines_ready = sem("sines_ready")
        var_ready = sem("var_ready")
        std_ready = sem("std_ready")
        shift_ready = sem("shift_ready")
        normed_dve = sem("normed_dve")
        normed_act = sem("normed_act")
        stored = sem("result_stored")
        block = ctx.enter_context(nc.Block())

        def slot(h, t):
            return out_banks[:, h, t * SLOT:t * SLOT + outs]

        @block.sync
        def _(sp):
            def load(g, h):
                for t in range(G):
                    if layer == 0:
                        sp.dma_start(blocks[:, h, t, :, MUL1:],
                                     total.rearrange("(t p d) f -> t p d f", p=P, d=NY)[bass.ds(g * G + t, 1)].rearrange(
                                         "t p d f -> p (t d) f")).then_inc(sums_in[h], 16)
                    else:
                        sp.dma_start(sums[:, h, t, :, :],
                                     total.rearrange("(t p d) f -> t p d f", p=P, d=NY)[bass.ds(g * G + t, 1)].rearrange(
                                         "t p d f -> p (t d) f")).then_inc(sums_in[h], 16)

            load(0, 0)
            load(1, 1)
            with sp.Fori(0, NG // 2 - 1) as i:
                for h in range(2):
                    g = i * 2 + h
                    if layer == 0:
                        sp.wait_ge(turned_in_psum, (g + 1) * G)
                    else:
                        sp.wait_ge(copied, g + 1)
                        sp.wait_ge(combined, g + 1)
                    load(g + 2, h)
            with sp.Fori(0, NG) as g:
                sp.wait_ge(normed_dve, g * (G - 2) + (G - 2))
                sp.wait_ge(normed_act, g * 2 + 2)
                sp.dma_start(result.rearrange("(t p) f -> p t f", p=P)[:, bass.ds(g * G, G), :],
                             x[:, bass.ds(g * G, G), :]).then_inc(stored, 16)
            sp.wait_ge(stored, 16 * NG)

        @block.gpsimd
        def _(pool):
            with pool.Fori(0, NG // 2) as i:
                for h in range(2):
                    g = i * 2 + h
                    pool.wait_ge(sums_in[h], (i + 1) * (16 * G))
                    if layer == 1:
                        pool.wait_ge(group_read, g + 1)
                    pool.sem_inc(copies_begun, 1)
                    if layer == 0:
                        nc.gpsimd.tensor_copy(
                            blocks[:, h, :, 1:, 0:MUL1],
                            blocks[:, h, :, 0, MUL1 + MUL0:].rearrange("p t (c u) -> p t c u", c=3)).then_inc(copied, 1)
                    else:
                        nc.gpsimd.tensor_copy(blocks[:, h, :, :, 0:MUL0], sums[:, h, :, :, 0:MUL0])
                        nc.gpsimd.tensor_copy(
                            blocks[:, h, :, 1:, MUL0:MUL0 + MUL1],
                            sums[:, h, :, 0, MUL0:].rearrange("p t (u c) -> p t c u", c=3)).then_inc(copied, 1)

        @block.tensor
        def _(pe):
            def turn(h, u, n):
                t = u % G
                pe.wait_ge(turned_out, n + 1)
                for d in range(NY):
                    mm = pe.transpose(turn_banks[0:span[d], u % 2, d * P:(d + 1) * P],
                                      blocks[:, h, t, d, 0:span[d]], keep["identity"][:])
                mm.then_inc(turned_in_psum, 1)

            def group_ready(g):
                pe.wait_ge(copied, g + 1)
                pe.wait_ge(combined, g + 1)

            with pe.Fori(0, NG // 2) as i:
                for u in range(2 * G):
                    h, t = divmod(u, G)
                    n = i * (2 * G) + u
                    if t == 0:
                        group_ready(i * 2 + h)
                        turn(h, u, n)
                    if t < G - 1:
                        turn(h, u + 1, n + 1)
                    if t == 0:
                        pe.wait_ge(group_read, i * 2 + h + 1)
                    pe.wait_ge(turned_out, n + 3)
                    out = slot(h, t)
                    first = outs - D
                    ws, wv = (keep["out_s"], keep["out_v"]) if layer == 0 else (keep["mix_s"], keep["mix_v"])
                    pe.matmul(out[:, 0:first + MUL0], turned[0:span[0], u % 2, 0, :], ws[:], start=True, stop=True)
                    for c in range(3):
                        mm = pe.matmul(out[:, first + MUL0:].rearrange("p (w c) -> p c w", c=3)[:, c, :],
                                       turned[0:span[1 + c], u % 2, 1 + c, :], wv[:], start=True, stop=True)
                    mm.then_inc(mapped, 1)

        @block.scalar
        def _(act):
            act.sem_inc(turned_out, 2)

            def make_relus(i, h):
                g = i * 2 + h
                act.wait_ge(mapped, (g + 1) * G + 2)
                act.wait_ge(group_read, g + 1)
                nc.scalar.activation(relus[:, h, :, :],
                                     out_banks[:, h, 0:G * SLOT].rearrange("p (t f) -> p t f", f=SLOT)[:, :, 0:D],
                                     ACT.Relu).then_inc(relus_made, 1)

            with act.Fori(0, NG // 2) as i:
                for u in range(2 * G):
                    h, t = divmod(u, G)
                    n = i * (2 * G) + u
                    act.wait_ge(turned_in_psum, n + 1)
                    act.wait_ge(mapped, n + 1)
                    if span[0] == span[1]:
                        nc.scalar.copy(turned[0:span[0], u % 2, :, :],
                                       turn_banks[0:span[0], u % 2, :].rearrange("p (d n) -> p d n", d=NY)
                                       ).then_inc(turned_out, 1)
                    else:
                        nc.scalar.copy(turned[0:span[0], u % 2, 0, :], turn_banks[0:span[0], u % 2, 0:P])
                        nc.scalar.copy(turned[0:span[1], u % 2, 1:, :],
                                       turn_banks[0:span[1], u % 2, P:].rearrange("p (d n) -> p d n", d=3)
                                       ).then_inc(turned_out, 1)
                    if layer == 1 and t == G - 1:
                        make_relus(i, h)
                    if layer == 0 and t == G - 1:
                        act.wait_ge(angles_ready, i * 2 + h + 1)
                        nc.scalar.activation(small[:, 6, :], small[:, 5, :], ACT.Sin).then_inc(sines_ready, 1)
            act.wait_ge(var_ready, 1)
            nc.scalar.activation(spreads[:, 1, :], spreads[:, 0, :], ACT.Sqrt).then_inc(std_ready, 1)
            act.wait_ge(shift_ready, 1)
            with act.Fori(0, NG) as g:
                for t in (G - 2, G - 1):
                    row = x[:, bass.ds(g * G + t, 1), :].rearrange("p t f -> p (t f)")
                    nc.scalar.activation(row, row, ACT.Identity, bias=spreads[:, 2, bass.ds(g * G + t, 1)],
                                         scale=spreads[:, 1, bass.ds(g * G + t, 1)]).then_inc(normed_act, 1)

        @block.vector
        def _(dve):
            dve.sem_inc(mapped, 2)
            dve.sem_inc(group_read, 2)
            vv = nc.vector

            def combine_blocks(i, h):
                dve.wait_ge(sums_in[h], (i + 1) * (16 * G))
                if layer == 0:
                    def part(c):
                        at = MUL1 + MUL0 + c * MUL1
                        return blocks[:, h, :, 1 + c, at:at + MUL1]
                    dve.wait_ge(copied, i * 2 + h + 1)
                    vv.tensor_tensor(blocks[:, h, :, 0, 0:MUL1], part(0), part(1), ALU.add)
                    dve.drain()
                    vv.tensor_tensor(blocks[:, h, :, 0, 0:MUL1], blocks[:, h, :, 0, 0:MUL1], part(2),
                                     ALU.add).then_inc(combined, 1)
                    return

                def moment(e, c):
                    return sums[:, h, :, 1 + e, MUL0:].rearrange("p t (u c) -> p t c u", c=3)[:, :, c, :]
                for c in range(3):
                    a, b = (c + 1) % 3, (c + 2) % 3
                    vv.tensor_tensor(blocks[:, h, :, 1 + c, MUL0 + MUL1:], moment(b, a), moment(a, b), ALU.subtract)
                dot = blocks[:, h, :, 0, MUL0:MUL0 + MUL1]
                vv.tensor_tensor(dot, moment(0, 0), moment(1, 1), ALU.add)
                dve.drain()
                vv.tensor_tensor(dot, dot, moment(2, 2), ALU.add).then_inc(combined, 1)

            def angles(g, h):
                attr = keep["attr"][:, bass.ds(g * G, G)]
                ang, turns, r, c = small[:, 0, 0:G], small[:, 1, 0:G], small[:, 5, 0:G], small[:, 5, G:]
                vv.tensor_tensor(ang, out_banks[:, h, 0:G * SLOT].rearrange("p (t f) -> p t f", f=SLOT)[:, :, 0],
                                 attr, ALU.mult)
                dve.drain()
                vv.tensor_scalar(turns, ang, float(1 / TURN), ROUND, ALU.mult, ALU.add)
                dve.drain()
                vv.tensor_scalar(turns, turns, -ROUND, None, ALU.add)
                dve.drain()
                vv.scalar_tensor_tensor(ang, turns, -TURN_HI, ang, ALU.mult, ALU.add)
                dve.drain()
                vv.scalar_tensor_tensor(ang, turns, -TURN_MID, ang, ALU.mult, ALU.add)
                dve.drain()
                vv.scalar_tensor_tensor(ang, turns, -TURN_LO, ang, ALU.mult, ALU.add)
                dve.drain()
                vv.tensor_scalar(small[:, 3, 0:G], ang, float(np.pi / 2), float(-TURN), ALU.is_gt, ALU.mult)
                vv.tensor_scalar(small[:, 4, 0:G], ang, float(np.pi / 2), None, ALU.add)
                vv.tensor_scalar(r, ang, PI_IN, -PI_IN, ALU.min, ALU.max)
                dve.drain()
                vv.tensor_tensor(c, small[:, 4, 0:G], small[:, 3, 0:G], ALU.add)
                dve.drain()
                vv.tensor_scalar(c, c, PI_IN, -PI_IN, ALU.min, ALU.max).then_inc(angles_ready, 1)
                dve.wait_ge(sines_ready, g + 1)
                vv.tensor_tensor(small[:, 7, 0:G], small[:, 6, 0:G], attr, ALU.mult)
                dve.drain()

            def finish_group(i, h):
                g = i * 2 + h
                dve.wait_ge(mapped, (g + 1) * G + 2)
                if layer == 0:
                    angles(g, h)
                for t in range(G):
                    if layer == 0:
                        row = x[:, bass.ds(g * G + t, 1), :].rearrange("p t f -> p (t f)")
                        vv.scalar_tensor_tensor(row, slot(h, t)[:, 1:], small[:, 7, t:t + 1], row,
                                                ALU.mult, ALU.add)
                if layer == 1:
                    dve.wait_ge(relus_made, g + 1)
                    rows = x[:, bass.ds(g * G, G), :].rearrange("p t f -> p (t f)")
                    vv.scalar_tensor_tensor(rows, rows, 2.0, relus[:, h, :, :].rearrange("p t f -> p (t f)"),
                                            ALU.mult, ALU.add)
                dve.drain().then_inc(group_read, 1)
                if layer == 0:
                    for t in range(G):
                        row = x[:, bass.ds(g * G + t, 1), :].rearrange("p t f -> p (t f)")
                        self_row = keep["sc"][:, bass.ds(g * G + t, 1), :].rearrange("p t f -> p (t f)")
                        vv.scalar_tensor_tensor(row, self_row, small[:, 6, G + t:G + t + 1], row,
                                                ALU.mult, ALU.add)
                    dve.drain()
                for t in range(G):
                    row = x[:, bass.ds(g * G + t, 1), :].rearrange("p t f -> p (t f)")
                    vv.bn_stats(stats6[:, t, :], row)
                dve.drain()
                for t in range(G):
                    vv.bn_aggr(stats2[:, t, :], stats6[:, t, :])
                dve.drain()
                vv.tensor_copy(stats[:, bass.ds(g * G, G), :], stats2[:])

            combine_blocks(0, 0)
            with dve.Fori(0, NG // 2 - 1) as i:
                combine_blocks(i, 1)
                finish_group(i, 0)
                combine_blocks(i + 1, 0)
                finish_group(i, 1)
            combine_blocks(NG // 2 - 1, 1)
            finish_group(NG // 2 - 1, 0)
            finish_group(NG // 2 - 1, 1)
            dve.drain()
            vv.tensor_scalar(spreads[:, 0, :], stats[:, :, 1], EPS, None, ALU.add).then_inc(var_ready, 1)
            dve.wait_ge(std_ready, 1)
            vv.reciprocal(spreads[:, 1, :], spreads[:, 1, :])
            dve.drain()
            vv.scalar_tensor_tensor(spreads[:, 2, :], stats[:, :, 0], -1.0, spreads[:, 1, :],
                                    ALU.mult, ALU.mult).then_inc(shift_ready, 1)
            dve.drain()
            with dve.Fori(0, NG) as g:
                for t in range(G - 2):
                    row = x[:, bass.ds(g * G + t, 1), :].rearrange("p t f -> p (t f)")
                    vv.tensor_scalar(row, row, spreads[:, 1, bass.ds(g * G + t, 1)],
                                     spreads[:, 2, bass.ds(g * G + t, 1)], ALU.mult, ALU.add).then_inc(normed_dve, 1)


def build(nc, io, out):
    with ExitStack() as ctx:
        def sb(name, shape, dt=F32):
            return ctx.enter_context(nc.sbuf_tensor(name, shape, dt))

        keep = {
            "x": sb("x_rows", [P, NT, D]),
            "sc": sb("self_rows", [P, NT, D]),
            "attr": sb("node_attr", [P, NT]),
            "src": sb("edge_src", [P, TILES + CH], I32),
            "dst": sb("edge_dst", [P, TILES]),
            "y": sb("edge_y", [P, TILES, NY]),
            "ranges": sb("ranges", [P, 2 * NCH], I32),
            "first_node": sb("first_node", [P, NCH]),
            "fc1": sb("fc1", [2 * RAD, 2 * HID]),
            "fc2": sb("fc2", [2 * HID, WNUM]),
            "out_s": sb("out_s", [MUL0 + MUL1, 1 + MUL0]),
            "out_v": sb("out_v", [MUL0 + MUL1, MUL1]),
            "mix_s": sb("mix_s", [MUL0 + MUL1, MUL0]),
            "mix_v": sb("mix_v", [MUL0 + 2 * MUL1, MUL1]),
            "node_of_column": sb("node_of_column", [P, P]),
            "identity": sb("identity", [P, P]),
            "harmonic_mask": sb("harmonic_mask", [P, 2]),
            "src_table": nc.dram_tensor("src_table", (NPAD, D), F32, kind="Internal").ap(),
            "x1_table": nc.dram_tensor("x1_table", (NPAD, D), F32, kind="Internal").ap(),
            "total0": nc.dram_tensor("total0", (NPAD * NY, D), F32, kind="Internal").ap(),
            "total1": nc.dram_tensor("total1", (NPAD * NY, D), F32, kind="Internal").ap(),
            "range_table": nc.dram_tensor("range_table", (1, 2 * NCH), I32, kind="Internal").ap(),
        }
        load_and_embed(nc, io, keep)
        sum_over_edges(nc, io, keep, 0)
        finish_nodes(nc, keep, 0, keep["x1_table"])
        sum_over_edges(nc, io, keep, 1)
        finish_nodes(nc, keep, 1, out)


def kernel(**inputs):
    import numpy as np
    import concourse.bacc as bacc
    from concourse.bass_utils import run_bass_kernel_spmd

    f = {name: np.asarray(a) for name, a in inputs.items()}

    def by_node(a):
        full = np.zeros((NPAD, a.shape[1]), a.dtype)
        full[:NODES] = a
        return np.ascontiguousarray(full.reshape(NT, P, -1).transpose(1, 0, 2))

    def by_edge(a, fill=0):
        full = np.full((EPAD, a.shape[1]), fill, a.dtype)
        full[:EDGES] = a
        return full

    def in_tiles(a):
        return np.ascontiguousarray(a.reshape(TILES, P, -1).transpose(1, 0, 2))

    x, y = f["x"], f["edge_attr_4"]
    x_t = np.zeros((D, NPAD), x.dtype)
    x_t[:MUL0, :NODES] = x[:, :MUL0].T
    x_t[MUL0:, :NODES] = x[:, MUL0:].reshape(NODES, MUL1, 3).transpose(2, 1, 0).reshape(3 * MUL1, NODES)
    dst = by_edge(f["dst"].astype(np.int32)[:, None], f["dst"][-1])
    arrays = {
        "x": by_node(x),
        "x_t": x_t,
        "attr": by_node(f["node_vec1"])[:, :, 0].copy(),
        "src": np.pad(in_tiles(by_edge(f["src"].astype(np.int32)[:, None]))[:, :, 0], ((0, 0), (0, CH))),
        "dst": in_tiles(dst)[:, :, 0].copy(),
        "dst_chunks": dst.reshape(NCH // 2, 2, CHUNK),
        "y": in_tiles(by_edge(y)),
        "radial_t": np.ascontiguousarray(by_edge(f["edge_attr_8"]).T),
        "mix_s_t": np.concatenate([f["L1_gnn_W1"].T, f["L1_gnn_W2"].T], axis=1),
        "mix_v_t": np.concatenate([f["L1_gnn_W3"].T, f["L1_gnn_W4"].T, f["L1_gnn_W5"].T], axis=1),
        "node_of_column": np.broadcast_to(np.arange(P, dtype=np.float32) // NY, (P, P)).copy(),
        "identity": np.eye(P, dtype=np.float32),
        "harmonic_mask": np.stack([np.arange(P) % NY == 0, np.arange(P) % NY != 0], axis=1).astype(np.float32),
    }
    for name in ("L0_gnn_W_sc_s", "L0_gnn_W_sc_v", "L0_gnn_W1_s", "L0_gnn_W1_v", "L0_gnn_W2_s", "L0_gnn_W2_v",
                 "L0_gnn_W3", "L0_gnn_fcW1", "L0_gnn_fcW2", "L1_gnn_Ws", "L1_gnn_Wv"):
        arrays[name] = np.ascontiguousarray(f[name])

    nc = bacc.Bacc("TRN2", target_bir_lowering=False, num_devices=1)
    io = {name: nc.dram_tensor(f"in_{name}", a.shape, mybir.dt.from_np(a.dtype), kind="ExternalInput").ap()
          for name, a in arrays.items()}
    out = nc.dram_tensor("out_rows", (NPAD, D), F32, kind="ExternalOutput").ap()
    build(nc, io, out)
    run = run_bass_kernel_spmd(nc, [{f"in_{name}": a for name, a in arrays.items()}], core_ids=[0])
    return run.results[0]["out_rows"][:NODES]
```

```python
from contextlib import ExitStack

import numpy as np

import concourse.bass as bass
from concourse import mybir

ALU = mybir.AluOpType
ACT = mybir.ActivationFunctionType
F32 = mybir.dt.float32
I32 = mybir.dt.int32
BF16 = mybir.dt.bfloat16
AX = mybir.AxisListType

P = 128
NODES, EDGES = 6250, 200000
MUL0, MUL1 = 64, 32
D = MUL0 + 3 * MUL1
NY = 4
RAD, HID = 8, 64
WNUM = 2 * MUL0 + 2 * MUL1

CH = 7
CHUNK = CH * P
NCH = -(-EDGES // CHUNK)
RING = 4
assert NCH % RING == 0
TILES = NCH * CH
EPAD = TILES * P
WIN = P // NY
FRONT = (CH + 1) // 2
SPAN = FRONT * P

G = 7
NT = -(-NODES // P)
NG = NT // G
PAIRS = [(a, b) for b in range(3) for a in range(3)]
TERMS = len(PAIRS) - 1
K_HALF = TERMS * RAD
assert 2 * K_HALF <= P
STEP_EDGES = RING * CHUNK
SUB = RAD * STEP_EDGES // P
XT_RING = 3
assert NG * G == NT and NG % XT_RING == 1
LOOPS = NCH // RING

ROW = NY * D
BLOCKS = ROW // P
PIECE = 512
TOTAL_ROWS = (LOOPS - 1) * PIECE
BATCH = 5
EARLY = 2
LATE = TOTAL_ROWS // PIECE - EARLY * BATCH
LATE_STEPS = -(-LATE // RING)
EARLY_NODES = EARLY * BATCH * PIECE // NY
assert TOTAL_ROWS >= (NODES + WIN) * NY

PROD = 2 * D
OUTS = (1 + D, D)

INV3, INV6 = 1 / np.sqrt(3.0), 1 / np.sqrt(6.0)
MIX = 1 / np.sqrt(MUL0 + MUL1)
C1 = np.sqrt(3.0 / (MUL0 + 2 * MUL1))
LIN_S, LIN_V = 1 / np.sqrt(MUL0), 1 / np.sqrt(MUL1)
NEIGHBORS = 10.0
EPS = 1e-5

TURN = 2 * np.pi
TURN_HI = 6.28125
TURN_MID = float(np.float32(TURN - TURN_HI))
TURN_LO = float(TURN - TURN_HI - TURN_MID)
ROUND = 1.5 * 2.0**23
PI_IN = 3.1415925


def split_in_three(nc, dve, value, rest, parts):
    nc.vector.tensor_copy(parts[:, 0, :], value)
    dve.drain()
    nc.vector.tensor_tensor(rest, value, parts[:, 0, :], ALU.subtract)
    dve.drain()
    nc.vector.tensor_copy(parts[:, 1, :], rest)
    dve.drain()
    nc.vector.tensor_tensor(rest, rest, parts[:, 1, :], ALU.subtract)
    dve.drain()
    return nc.vector.tensor_copy(parts[:, 2, :], rest)


def store_parts(eng, keep, i, b, parts, stored):
    eng.dma_start(keep["radial_parts"].rearrange("(l a p j) -> l p a j", a=3, p=P, j=SUB)[
        bass.ds(i * 3 + b, 1)].rearrange("l p a j -> (l p) a j"), parts).then_inc(stored, 16)


def load_and_embed(nc, io, keep):
    with ExitStack() as ctx:
        def sb(name, shape, dt=F32):
            return ctx.enter_context(nc.sbuf_tensor(name, shape, dt))

        def sem(name):
            return ctx.enter_context(nc.semaphore(name))

        xt_a = sb("xt_a", [P, XT_RING, G * P])
        xt_b = sb("xt_b", [MUL1, XT_RING, G * P])
        embed_a = sb("embed_a", [P, 2, P])
        embed_b = sb("embed_b", [MUL1, 2, MUL1])
        map0_scale = sb("map0_scale", [P, BLOCKS, 1])
        dst_int = sb("dst_int", [P, TILES], I32)
        dst_chunks = sb("dst_chunks", [NCH // 2, 2, CHUNK], I32)
        warm = sb("warm", [P, 1])
        raw = sb("first_raw", [P, 2 * SUB])
        rest = sb("first_rest", [P, 2 * SUB])
        parts = sb("first_parts", [P, 3, 2 * SUB], BF16)
        fc1_rows = sb("fc1_rows", [P, 2 * HID])
        fc1_masks = sb("fc1_masks", [P, 3])
        fc1_rest = sb("fc1_rest", [P, 2 * HID])
        fc1_parts = sb("fc1_parts", [P, 3, 2 * HID], BF16)
        range_rows = sb("range_rows", [NCH // 2, 2, 2], I32)
        least = sb("least", [P, 2, 2 * LOOPS])
        banks = ctx.enter_context(nc.psum_tensor("embed_banks", [P, G, 512], F32))

        embed_in = sem("embed_in")
        embed_scaled = sem("embed_scaled")
        weights_in = sem("weights_in")
        attr_in = sem("attr_in")
        xt_in = [sem(f"xt_in_slot{h}_") for h in range(XT_RING)]
        embedded = sem("embedded")
        rows_out = sem("rows_out")
        self_out = sem("self_out")
        rows_stored = sem("rows_stored")
        zeros_made = sem("zeros_made")
        chunks_in = sem("chunks_in")
        ranges_made = sem("ranges_made")
        ranges_stored = sem("ranges_stored")
        ranges_in = sem("ranges_in")
        dst_in = sem("dst_in")
        src_in = sem("src_in")
        y_front_in = sem("y_front_in")
        raw_in = sem("first_raw_in")
        split = sem("first_split")
        parts_stored = sem("first_parts_stored")
        block = ctx.enter_context(nc.Block())

        weights = (("map0", keep["map0"]), ("map0_scale", map0_scale), ("fc1_rows", fc1_rows), ("fc1_masks", fc1_masks), ("fc2", keep["fc2"]),
                   ("window_nodes", keep["window_nodes"]), ("identity", keep["identity"]),
                   ("harmonic_mask", keep["harmonic_mask"]))

        @block.sync
        def _(sp):
            def load_columns(g):
                h, cols = g % XT_RING, slice(g * (G * P), (g + 1) * (G * P))
                sp.dma_start(xt_a[:, h, :], io["x_t"][0:P, cols]).then_inc(xt_in[h], 16)
                sp.dma_start(xt_b[:, h, :], io["x_t"][P:D, cols]).then_inc(xt_in[h], 16)

            def clear(k):
                rows = keep["total0"][k * (BATCH * PIECE):(k + 1) * (BATCH * PIECE), :]
                sp.dma_start(rows.rearrange("(k p r) f -> p k (r f)", p=P, r=PIECE // P),
                             keep["zeros"][:].unsqueeze(1).broadcast_to([P, BATCH, PIECE // P * D])
                             ).then_inc(keep["early_zeros"], 16)

            sp.dma_start(embed_a[:], io["embed_a"]).then_inc(embed_in, 16)
            sp.dma_start(embed_b[:], io["embed_b"]).then_inc(embed_in, 16)
            load_columns(0)
            sp.dma_start(keep["attr"][:], io["attr"]).then_inc(attr_in, 16)
            load_columns(1)
            load_columns(2)
            for name, place in weights:
                sp.dma_start(place[:], io[name]).then_inc(weights_in, 16)
            for i in range(2):
                sp.dma_start(raw[:, i * SUB:(i + 1) * SUB], io["radial"][i]).then_inc(raw_in, 16)
            for g in range(XT_RING, NG):
                sp.wait_ge(embedded, (g - XT_RING + 1) * G)
                load_columns(g)
            sp.wait_ge(split, 1)
            for i in range(2):
                for b in range(3):
                    store_parts(sp, keep, i, b, parts[:, :, i * SUB:(i + 1) * SUB], parts_stored)
            sp.wait_ge(zeros_made, 1)
            clear(0)
            sp.wait_ge(rows_stored, 16 * NG)
            for k in range(1, EARLY):
                clear(k)
            sp.dma_start(keep["y"][:, TILES // 2:, :], io["y"][:, TILES // 2:, :]).then_inc(keep["y_in"], 16)
            sp.wait_ge(parts_stored, 32 * 3)

        @block.tensor
        def _(pe):
            pe.wait_ge(embed_scaled, 2)

            def embed_group(g, i, h):
                pe.wait_ge(xt_in[h], i * 32 + 32)
                for t in range(G):
                    pe.wait_ge(self_out, g * G + (t + 1))
                    out = banks[:, t, 0:2 * D].rearrange("p (a f) -> p a f", a=2)
                    cols = slice(t * P, t * P + P)
                    pe.matmul(out[:, :, 0:P], xt_a[:, h, cols], embed_a[:], start=True, stop=True)
                    pe.matmul(out[:, :, P:], xt_b[:, h, cols], embed_b[:], start=True, stop=True).then_inc(embedded, 1)

            with pe.Fori(0, NG // XT_RING) as i:
                for h in range(XT_RING):
                    embed_group(i * XT_RING + h, i, h)
            embed_group(NG - 1, NG // XT_RING, 0)

        @block.scalar
        def _(act):
            act.wait_ge(zeros_made, 1)
            nc.scalar.activation(warm[:], keep["zeros"][:, 0:1], ACT.Copy)
            act.wait_ge(attr_in, 16)
            with act.Fori(0, NG) as g:
                for t in range(G):
                    n = g * G + t
                    act.wait_ge(embedded, n + 1)
                    nc.scalar.activation(keep["rows"][:, bass.ds(n, 1), :].rearrange("p t f -> p (t f)"),
                                         banks[:, t, 0:D], ACT.Copy, scale=keep["attr"][:, bass.ds(n, 1)]
                                         ).then_inc(rows_out, 1)
                act.wait_ge(rows_out, g * G + G)
                act.dma_start(keep["src_table"].rearrange("(t p) f -> p t f", p=P)[:, bass.ds(g * G, G), :],
                              keep["rows"][:, bass.ds(g * G, G), :]).then_inc(rows_stored, 16)
            act.wait_ge(rows_stored, 16 * NG)

        @block.vector
        def _(dve):
            nc.vector.memset(keep["zeros"][:], 0.0).then_inc(zeros_made, 1)
            nc.vector.memset(least[:], float(NODES))
            dve.sem_inc(self_out, G)
            dve.wait_ge(embed_in, 32)
            nc.vector.tensor_scalar(embed_a[0:MUL0], embed_a[0:MUL0], float(LIN_S), None, ALU.mult)
            nc.vector.tensor_scalar(embed_a[MUL0:], embed_a[MUL0:], float(LIN_V), None,
                                    ALU.mult).then_inc(embed_scaled, 1)
            nc.vector.tensor_scalar(embed_b[:], embed_b[:], float(LIN_V), None, ALU.mult).then_inc(embed_scaled, 1)
            dve.wait_ge(chunks_in, 16)
            nc.vector.tensor_reduce(range_rows[:, :, 0], dst_chunks[:], AX.X, ALU.min)
            nc.vector.tensor_reduce(range_rows[:, :, 1], dst_chunks[:], AX.X, ALU.max).then_inc(ranges_made, 1)
            dve.wait_ge(attr_in, 16)

            def take_self(groups):
                with dve.Fori(*groups) as g:
                    for t in range(G):
                        n = g * G + t
                        dve.wait_ge(rows_out, n + 1)
                        nc.vector.tensor_scalar(keep["sc"][:, bass.ds(n, 1), :].rearrange("p t f -> p (t f)"),
                                                banks[:, t, D:2 * D], keep["attr"][:, bass.ds(n, 1)], None,
                                                ALU.mult).then_inc(self_out, 1)

            take_self((0, 2))
            dve.wait_ge(raw_in, 32)
            split_in_three(nc, dve, raw[:], rest[:], parts).then_inc(split, 1)
            take_self((2, 3))
            dve.wait_ge(ranges_in, 16)
            nc.vector.tensor_copy(keep["first_node"][:], keep["ranges"][:].rearrange("p (c r) -> p c r", r=2)[:, :, 0])
            dve.drain()
            nc.vector.tensor_reduce(least[:, 0, 0:LOOPS], keep["first_node"][:].rearrange("p (l r) -> p l r", r=RING),
                                    AX.X, ALU.min)
            reach, at = 1, 0
            while reach < LOOPS:
                dve.drain()
                nc.vector.tensor_tensor(least[:, 1 - at, 0:LOOPS], least[:, at, 0:LOOPS],
                                        least[:, at, reach:reach + LOOPS], ALU.min)
                reach, at = 2 * reach, 1 - at
            for first, then in ((1 / P, -(P - 1) / (2 * P)), (1.0, ROUND), (1.0, -ROUND)):
                dve.drain()
                nc.vector.tensor_scalar(least[:, at, 0:LOOPS], least[:, at, 0:LOOPS], first, then, ALU.mult, ALU.add)
            dve.drain()
            nc.vector.tensor_copy(keep["ready"][:], least[:, at, 0:LOOPS])
            take_self((3, 4))
            dve.wait_ge(dst_in, 16)
            nc.vector.tensor_copy(keep["dst"][:], dst_int[:])
            take_self((4, 5))
            dve.wait_ge(weights_in, 16 * len(weights))
            nc.vector.tensor_scalar(keep["fc2"][:], keep["fc2"][:], float(1 / np.sqrt(HID)), None, ALU.mult)
            split_in_three(nc, dve, fc1_rows[:], fc1_rest[:], fc1_parts)
            dve.drain()
            nc.vector.tensor_scalar(fc1_rows[:], fc1_parts[:, 0, :], fc1_masks[:, 0:1], None, ALU.mult)
            dve.drain()
            nc.vector.scalar_tensor_tensor(fc1_rows[:], fc1_parts[:, 1, :], fc1_masks[:, 1:2], fc1_rows[:],
                                           ALU.mult, ALU.add)
            dve.drain()
            nc.vector.scalar_tensor_tensor(keep["fc1"][:], fc1_parts[:, 2, :], fc1_masks[:, 2:3], fc1_rows[:],
                                           ALU.mult, ALU.add)
            nc.vector.tensor_tensor(keep["map0"][:], keep["map0"][:],
                                    map0_scale[:].broadcast_to([P, BLOCKS, OUTS[0]]), ALU.mult)
            dve.drain()
            nc.vector.tensor_scalar(keep["map0"][:, :, 0:1], keep["map0"][:, :, 0:1], 0.1, None, ALU.mult)
            take_self((5, NG))

        @block.gpsimd
        def _(pool):
            pool.dma_start(dst_chunks[:], io["dst_chunks"]).then_inc(chunks_in, 16)
            pool.dma_start(keep["src"][:], io["src"]).then_inc(src_in, 16)
            pool.dma_start(dst_int[:], io["dst"]).then_inc(dst_in, 16)
            pool.wait_ge(ranges_made, 1)
            pool.dma_start(keep["range_table"].rearrange("a (p q) -> (a p) q", q=4),
                           range_rows[:].rearrange("p a b -> p (a b)")).then_inc(ranges_stored, 16)
            pool.wait_ge(ranges_stored, 16)
            pool.dma_start(keep["ranges"][:], keep["range_table"].broadcast_to([P, 2 * NCH])).then_inc(ranges_in, 16)
            pool.wait_ge(embedded, 3 * G)
            pool.dma_start(keep["y"][:, 0:TILES // 2, :], io["y"][:, 0:TILES // 2, :]).then_inc(y_front_in, 16)
            pool.wait_ge(y_front_in, 16)
            pool.wait_ge(src_in, 16)
            pool.wait_ge(dst_in, 16)
            pool.wait_ge(ranges_in, 16)


def sum_over_edges(nc, io, keep, layer, result=None):
    weighted = layer == 0
    table = keep["src_table"] if weighted else keep["x1_table"]
    total = keep["total0"] if weighted else keep["total1"]
    width = PROD if weighted else D
    with ExitStack() as ctx:
        def sb(name, shape, dt=F32):
            return ctx.enter_context(nc.sbuf_tensor(f"{name}{layer}", shape, dt))

        def sem(name):
            return ctx.enter_context(nc.semaphore(f"{name}{layer}"))

        def psum(name, shape):
            return ctx.enter_context(nc.psum_tensor(f"{name}{layer}", shape, F32))

        gathered = sb("gathered", [P, RING, CH, D])
        indices = sb("indices", [P, RING, CH], I32)
        spread = sb("spread", [P, 2, CH, P])
        chosen = sb("chosen", [P, 2, CH, WIN])
        base = sb("base", [P, 1])
        slab = sb("slab", [P, D])
        sums = sb("sums", [P, ROW])
        turned = sb("turned", [P, ROW])
        relus = sb("relus", [P, D])
        stats6 = sb("stats6", [P, 6])
        moments = sb("moments", [P, 2])
        norm = sb("norm", [P, 4])
        window = psum("window", [P, 512])
        turn_bank = psum("turn_bank", [P, 512])
        map_bank = psum("map_bank", [P, 512])
        if weighted:
            product = sb("product", [P, 2, CH, PROD])
            radial = sb("radial", [2 * K_HALF, 2, SPAN], BF16)
            raw = sb("raw", [P, SUB])
            rest = sb("rest", [P, SUB])
            parts = sb("parts", [P, 3, SUB], BF16)
            hidden = sb("hidden", [2 * HID, SPAN])
            hid_bank = psum("hid_bank", [2 * HID, 512])
            w_banks = psum("w_banks", [P, 4, 512])

        rows_in = [sem(f"rows_in_slot{q}_") for q in range(RING)]
        indices_ready = sem("indices_ready")
        gathers_begun = sem("gathers_begun")
        radial_in = [sem("radial_in_even"), sem("radial_in_odd")]
        hid_ready = sem("hid_ready")
        hid_active = sem("hid_active")
        w_ready = sem("w_ready")
        w_used = sem("w_used")
        chunk_summed = sem("chunk_summed")
        spread_ready = sem("spread_ready")
        more_spread = sem("more_spread")
        window_ready = sem("window_ready")
        window_added = sem("window_added")
        slab_in = sem("slab_in")
        slab_stored = sem("slab_stored")
        all_stored = sem("all_stored")
        late_rows_seen = sem("late_rows_seen")
        totals_complete = sem("totals_complete")
        sums_in = sem("sums_in")
        transposed = sem("transposed")
        turned_out = sem("turned_out")
        mapped = sem("mapped")
        results_out = sem("results_out")
        relus_used = sem("relus_used")
        var_ready = sem("var_ready")
        std_ready = sem("std_ready")
        normed = sem("normed")
        result_stored = sem("result_stored")
        late_zeros = sem("late_zeros")
        next_zeros = sem("next_zeros")
        x_in = sem("x_in")
        raw_in = sem("raw_in")
        split = sem("split")
        parts_stored = sem("parts_stored")
        block = ctx.enter_context(nc.Block())
        node_map = keep["map0"] if weighted else keep["map1"]
        outs = OUTS[layer]
        results = map_bank[:, P:P + outs]
        banks_of = [[0, 1], [4, 5], [6], [2, 3]]
        NB = len(banks_of)

        def node_counter(eng, name):
            counter = eng.alloc_register(f"{name}{layer}")
            eng.reg_mov(counter, 0)
            return counter

        def tile_of(eng, counter):
            return eng.snap(counter, min_val=0, max_val=NT - 1)

        def if_ready(eng, i, counter, work):
            ready = eng.value_load(keep["ready"][0:1, bass.ds(i, 1)])
            tile = tile_of(eng, counter)
            with eng.If(ready > tile):
                work(tile)
                eng.reg_add(counter, counter, 1)

        def if_begun(eng, begun, counter, work):
            first, tile = eng.snap(begun), tile_of(eng, counter)
            with eng.If(first > tile):
                work(tile)
                eng.reg_add(counter, counter, 1)

        def over_rest(eng, counter, *works):
            with eng.Fori(tile_of(eng, counter), NT) as tile:
                for work in works:
                    work(tile)

        def over_chunks(eng, step):
            with eng.Fori(0, NCH // RING - 1) as i:
                for h in range(RING):
                    step(i * RING + h, i, h)
            for h in range(RING):
                step(NCH - RING + h, NCH // RING - 1, h)

        def is_last(c, ahead):
            return isinstance(c, int) and c + ahead >= NCH

        def lap(i, h, ring):
            return i * (RING // ring) + (h // ring + 1)

        def bounds(eng, c, addressed=False):
            known = dict(min_val=0, max_val=NODES - 1) if addressed else {}
            lo = eng.value_load(keep["ranges"][0:1, bass.ds(c * 2, 1)], **known)
            hi = eng.value_load(keep["ranges"][0:1, bass.ds(c * 2 + 1, 1)], **known)
            return lo, hi

        def stage_indices(copy, c, h):
            copy(indices[:, h, :], keep["src"][:, bass.ds(c * CH, CH)]).then_inc(indices_ready, 1)

        @block.gpsimd
        def _(pool):
            def gather(c, h):
                pool.wait_ge(indices_ready, c + 1)
                pool.sem_inc(gathers_begun, 1)
                for k in range(CH):
                    pool.indirect_dma_start(
                        gathered[:, h, k, :], None, table,
                        bass.IndirectOffsetOnAxis(indices[:, h, k:k + 1], axis=0),
                    ).then_inc(rows_in[h], 16)

            for c in range(RING):
                gather(c, c)

            def gather_ahead(c, i, h):
                if is_last(c, RING):
                    return
                if weighted:
                    pool.wait_ge(w_used, (c + 1) * NB)
                else:
                    pool.wait_ge(chunk_summed, c + 1)
                gather(c + RING, h)

            over_chunks(pool, gather_ahead)

        @block.sync
        def _(sp):
            passes = sp.alloc_register(f"sp_passes{layer}")
            sp.reg_mov(passes, 0)
            if weighted:
                sp.wait_ge(keep["early_zeros"], 16 * EARLY)
            sp.dma_start(slab[:], total[0:P, :]).then_inc(slab_stored, 16)
            begun = node_counter(sp, "sp_begun")

            def load_node(tile):
                n = sp.snap(passes)
                sp.wait_ge(slab_stored, n * 16 + 16)
                sp.sem_inc(totals_complete, 1)
                sp.wait_ge(transposed, tile + 1)
                sp.dma_start(sums[:], total[0:NT * P * NY, :].rearrange("(t p d) f -> t p (d f)", p=P, d=NY)[
                    bass.ds(tile, 1)].rearrange("t p f -> p (t f)")).then_inc(sums_in, 16)

            cleared = sp.alloc_register(f"sp_cleared{layer}")
            sp.reg_mov(cleared, 0)

            def clear(piece):
                sp.dma_start(total[bass.ds((piece + EARLY * BATCH) * PIECE, PIECE), :].rearrange(
                    "(p r) f -> p (r f)", p=P), keep["zeros"][:]).then_inc(late_zeros, 16)

            def next_piece():
                return sp.snap(cleared, min_val=0, max_val=LATE - 1)

            def add_windows(c, early=False):
                lo, hi = bounds(sp, c, addressed=True)
                if early:
                    with sp.If(sp.snap(cleared) < LATE):
                        clear(next_piece())
                        sp.reg_add(cleared, cleared, 1)
                    with sp.If(hi >= EARLY_NODES - WIN):
                        with sp.If(sp.snap(cleared) < LATE):
                            with sp.Fori(next_piece(), LATE) as piece:
                                clear(piece)
                            sp.reg_mov(cleared, LATE)
                        sp.wait_ge(late_zeros, 16 * LATE)
                        sp.sem_inc(late_rows_seen, 1)
                with sp.Fori(lo, hi + 1, WIN) as base:
                    n = sp.snap(passes)
                    rows = total[bass.ds(base * NY, P), :]
                    sp.wait_ge(slab_stored, n * 16 + 16)
                    sp.dma_start(slab[:], rows).then_inc(slab_in, 16)
                    sp.wait_ge(window_added, n + 2)
                    sp.dma_start(rows, slab[:]).then_inc(slab_stored, 16)
                    sp.reg_add(passes, passes, 1)

            def loop_step(i, early=False):
                if_ready(sp, i, begun, load_node)
                for h in range(RING):
                    add_windows(i * RING + h, early)

            if weighted:
                with sp.Fori(0, LATE_STEPS) as i:
                    loop_step(i, early=True)
                sp.wait_ge(late_zeros, 16 * LATE)
            with sp.Fori(LATE_STEPS if weighted else 0, LOOPS) as i:
                loop_step(i)
            over_rest(sp, begun, load_node)
            n = sp.snap(passes)
            sp.wait_ge(slab_stored, n * 16 + 16)
            sp.sem_inc(all_stored, 1)

        @block.tensor
        def _(pe):
            def make_hidden(c, i, h):
                pe.wait_ge(radial_in[h % 2], lap(i, h, 2) * 16)
                if not (isinstance(c, int) and c == 0):
                    pe.wait_ge(hid_active, c)
                pe.matmul(hid_bank[:, 0:SPAN], keep["fc1"][:], radial[:, h % 2, :],
                          start=True, stop=True).then_inc(hid_ready, 1)

            def make_weights(c):
                pe.wait_ge(hid_active, c + 1)
                for banks, tiles in (((0, 1), (0, 4, 1, 5)), ((2, 3), (6, 2, 3))):
                    if not (isinstance(c, int) and c == 0):
                        pe.wait_ge(w_used, (c - 1) * NB + (banks[1] + 1))
                    for k in tiles:
                        b = next(b for b in banks if k in banks_of[b])
                        j = banks_of[b].index(k)
                        part = slice(0, HID) if k < FRONT else slice(HID, 2 * HID)
                        at = k % FRONT * P
                        mm = pe.matmul(w_banks[:, b, j * WNUM:(j + 1) * WNUM], hidden[part, at:at + P],
                                       keep["fc2"][part, :], start=True, stop=True)
                        if k == banks_of[b][-1]:
                            mm.then_inc(w_ready, 1)

            passes = pe.alloc_register(f"pe_passes{layer}")
            extra = pe.alloc_register(f"pe_extra{layer}")
            pe.reg_mov(passes, 0)
            pe.reg_mov(extra, 0)

            def sum_window(h, n, made, count):
                pe.wait_ge(window_added, n + 1)
                pe.wait_ge(made, count + 1)
                for k in range(CH):
                    mm = pe.matmul(window[:, 0:width], spread[:, h % 2, k, :],
                                   product[:, h % 2, k, :] if weighted else gathered[:, h, k, :],
                                   start=(k == 0), stop=(k == CH - 1))
                mm.then_inc(window_ready, 1)
                pe.reg_add(passes, passes, 1)

            def sum_windows(c, i, h):
                if not weighted:
                    pe.wait_ge(rows_in[h], lap(i, h, RING) * (16 * CH))
                sum_window(h, pe.snap(passes), spread_ready, c)
                lo, hi = bounds(pe, c)
                with pe.If(hi - lo >= WIN):
                    with pe.Fori(lo + WIN, hi + 1, WIN):
                        sum_window(h, pe.snap(passes), more_spread, pe.snap(extra))
                        pe.reg_add(extra, extra, 1)

            def turn_node(tile):
                pe.wait_ge(sums_in, tile * 16 + 16)
                pe.wait_ge(results_out, tile + 1)
                for k in range(BLOCKS):
                    out = turn_bank[:, k * P:(k + 1) * P] if k < BLOCKS - 1 else map_bank[:, 0:P]
                    mm = pe.transpose(out, sums[:, k * P:(k + 1) * P], keep["identity"][:])
                mm.then_inc(transposed, 1)

            def map_node(tile):
                pe.wait_ge(turned_out, tile + 1)
                for k in range(BLOCKS):
                    mm = pe.matmul(results, turned[:, k * P:(k + 1) * P], node_map[:, k, :],
                                   start=(k == 0), stop=(k == BLOCKS - 1))
                mm.then_inc(mapped, 1)

            begun, done = node_counter(pe, "pe_begun"), node_counter(pe, "pe_done")
            pe.sem_inc(transposed, 1)
            if weighted:
                make_hidden(0, 0, 0)
                make_weights(0)
                make_hidden(1, 0, 1)

            def step(c, i, h):
                if weighted and not is_last(c, 1):
                    make_weights(c + 1)
                if weighted and not is_last(c, 2):
                    make_hidden(c + 2, i, h + 2)
                sum_windows(c, i, h)
                if h == 1:
                    if_ready(pe, i, begun, turn_node)
                if h == 2:
                    if_begun(pe, begun, done, map_node)

            over_chunks(pe, step)
            over_rest(pe, begun, turn_node, map_node)

        @block.scalar
        def _(act):
            def turn_out(tile):
                act.wait_ge(transposed, tile + 2)
                nc.scalar.copy(turned[:, 0:512], turn_bank[:])
                nc.scalar.copy(turned[:, 512:], map_bank[:, 0:P]).then_inc(turned_out, 1)

            def take_results(tile):
                act.wait_ge(mapped, tile + 1)
                if weighted:
                    nc.scalar.copy(keep["rows"][:, bass.ds(tile, 1), :].rearrange("p t f -> p (t f)"), results[:, 1:])
                    nc.scalar.copy(keep["angle"][:, bass.ds(tile, 1)], results[:, 0:1]).then_inc(results_out, 1)
                else:
                    act.wait_ge(relus_used, tile + 1)
                    nc.scalar.activation(relus[:], results, ACT.Relu).then_inc(results_out, 1)

            begun, done = node_counter(act, "act_begun"), node_counter(act, "act_done")
            act.sem_inc(results_out, 1)
            if not weighted:
                closed = node_counter(act, "act_closed")

                def close_node(tile):
                    act.wait_ge(var_ready, tile + 1)
                    nc.scalar.activation(norm[:, 1:2], norm[:, 0:1], ACT.Sqrt).then_inc(std_ready, 1)
                    act.wait_ge(normed, tile + 1)
                    act.dma_start(result.rearrange("(t p) f -> p t f", p=P)[:, bass.ds(tile, 1), :],
                                  keep["rows"][:, bass.ds(tile, 1), :]).then_inc(result_stored, 16)

                for c in range(RING):
                    stage_indices(nc.scalar.copy, c, c)

                def stage_ahead(c, i, h):
                    if not is_last(c, RING):
                        act.wait_ge(rows_in[h], lap(i, h, RING) * (16 * CH))
                        stage_indices(nc.scalar.copy, c + RING, h)
                    if h == 1:
                        if_ready(act, i, begun, turn_out)
                    if h == 2:
                        if_begun(act, begun, done, take_results)
                    if h == 3:
                        if_begun(act, begun, closed, close_node)

                over_chunks(act, stage_ahead)
                over_rest(act, begun, turn_out, take_results, close_node)
                act.wait_ge(result_stored, 16 * NT)
                return

            def load_radial(i, h):
                i, h = i + h // RING, h % RING
                if h == 0 and not isinstance(i, int):
                    act.wait_ge(parts_stored, i * 48)
                at = i * (len(PAIRS) * RAD * STEP_EDGES) + h * CHUNK
                rows = keep["radial_parts"][bass.ds(at, K_HALF * STEP_EDGES)].rearrange("(k e) -> k e", e=STEP_EDGES)
                act.dma_start(radial[:, h % 2, :],
                              rows[:, 0:2 * SPAN].rearrange("k (b e) -> b k e", b=2)).then_inc(radial_in[h % 2], 16)

            load_radial(0, 0)
            load_radial(0, 1)

            def activate(c, i, h):
                if not (isinstance(c, int) and c == 0):
                    act.wait_ge(w_ready, c * NB)
                act.wait_ge(hid_ready, c + 1)
                nc.scalar.activation(hidden[:], hid_bank[:, 0:SPAN], ACT.Silu,
                                     scale=float(1 / np.sqrt(RAD))).then_inc(hid_active, 1)
                if not is_last(c, 2):
                    load_radial(i, h + 2)

            def loop_step(i, group=None):
                if group is not None:
                    act.dma_start(keep["x"][:, bass.ds(group * G, G), :],
                                  io["x"][:, bass.ds(group * G, G), :]).then_inc(x_in, 16)
                act.dma_start(raw[:], io["radial"].rearrange("l p j -> p l j")[:, bass.ds(i + 2, 1), :].rearrange(
                    "p l j -> p (l j)")).then_inc(raw_in, 16)
                for h in range(1, RING + 1):
                    activate(i * RING + h, i, h)
                    if h == 2:
                        act.dma_start(keep["total1"][bass.ds(i * PIECE, PIECE), :].rearrange("(p r) f -> p (r f)", p=P),
                                      keep["zeros"][:]).then_inc(next_zeros, 16)
                    if h == 2:
                        act.wait_ge(split, i + 1)
                    if h >= 2:
                        store_parts(act, keep, i + 2, h - 2, parts[:], parts_stored)
                    if h == 3:
                        if_ready(act, i, begun, turn_out)
                    if h == 4:
                        if_begun(act, begun, done, take_results)

            activate(0, 0, 0)
            with act.Fori(0, NG) as i:
                loop_step(i, group=i)
            with act.Fori(NG, LOOPS - 1) as i:
                loop_step(i)
            act.wait_ge(parts_stored, 48 * LOOPS)
            for h in range(1, RING):
                activate(NCH - RING + h, LOOPS - 1, h)
            if_ready(act, LOOPS - 1, begun, turn_out)
            if_begun(act, begun, done, take_results)
            over_rest(act, begun, turn_out, take_results)
            act.wait_ge(next_zeros, 16 * (LOOPS - 1))
            act.wait_ge(x_in, 16 * NG)

        @block.vector
        def _(dve):
            passes = dve.alloc_register(f"dve_passes{layer}")
            dve.reg_mov(passes, 0)

            def weigh(c, i, h):
                slot, half = h % RING, h % 2
                dve.wait_ge(rows_in[slot], lap(i, h, RING) * (16 * CH))
                if not is_last(c, RING):
                    stage_indices(nc.vector.tensor_copy, c + RING, slot)
                for b, tiles in enumerate(banks_of):
                    m, pair = len(tiles), slice(tiles[0], tiles[-1] + 1)
                    dve.wait_ge(w_ready, c * NB + b + 1)
                    w = w_banks[:, b, 0:m * WNUM].rearrange("p (t w) -> p t w", t=m)
                    nc.vector.tensor_tensor(
                        product[:, half, pair, :].rearrange("p t (a f) -> p t a f", a=2)[:, :, :, 0:MUL0],
                        w[:, :, 0:2 * MUL0].rearrange("p t (a f) -> p t a f", a=2),
                        gathered[:, slot, pair, 0:MUL0].unsqueeze(2).broadcast_to([P, m, 2, MUL0]), ALU.mult)
                    for j, k in enumerate(tiles):
                        last = nc.vector.tensor_tensor(
                            product[:, half, k, :].rearrange("p (a f) -> p a f", a=2)[:, :, MUL0:D].rearrange(
                                "p a (c u) -> p a c u", c=3),
                            w[:, j, 2 * MUL0:].rearrange("p (a u) -> p a u", a=2).unsqueeze(2).broadcast_to(
                                [P, 2, 3, MUL1]),
                            gathered[:, slot, k, MUL0:D].rearrange("p (c u) -> p c u", c=3).unsqueeze(1).broadcast_to(
                                [P, 2, 3, MUL1]), ALU.mult)
                    last.then_inc(w_used, 1)

            def make_spread(c, h, first, made):
                nc.vector.scalar_tensor_tensor(
                    chosen[:, h % 2, :, :], keep["dst"][:, bass.ds(c * CH, CH)].unsqueeze(2).broadcast_to([P, CH, WIN]), first,
                    keep["window_nodes"][:].unsqueeze(1).broadcast_to([P, CH, WIN]), ALU.subtract, ALU.is_equal)
                dve.drain()
                nc.vector.tensor_tensor(
                    spread[:, h % 2, :, :].rearrange("p k (n d) -> p k n d", d=NY),
                    chosen[:, h % 2, :, :].unsqueeze(3).broadcast_to([P, CH, WIN, NY]),
                    keep["y"][:, bass.ds(c * CH, CH), :].unsqueeze(2).broadcast_to([P, CH, WIN, NY]),
                    ALU.mult).then_inc(made, 1)

            def first_spread(c, h):
                make_spread(c, h, keep["first_node"][:, bass.ds(c, 1)], spread_ready)

            def add_window(n):
                dve.wait_ge(slab_in, n * 16 + 16)
                dve.wait_ge(window_ready, n + 1)
                if not weighted:
                    nc.vector.tensor_tensor(slab[:], window[:, 0:D], slab[:], ALU.add).then_inc(window_added, 1)
                else:
                    nc.vector.scalar_tensor_tensor(slab[:], window[:, 0:D], keep["harmonic_mask"][:, 0:1],
                                                   slab[:], ALU.mult, ALU.add)
                    dve.drain()
                    nc.vector.scalar_tensor_tensor(slab[:], window[:, D:PROD], keep["harmonic_mask"][:, 1:2],
                                                   slab[:], ALU.mult, ALU.add).then_inc(window_added, 1)
                dve.reg_add(passes, passes, 1)

            def sum_windows(c, h):
                lo, hi = bounds(dve, c)
                add_window(dve.snap(passes))
                with dve.If(hi - lo >= WIN):
                    nc.vector.tensor_copy(base[:], keep["first_node"][:, bass.ds(c, 1)])
                    with dve.Fori(lo + WIN, hi + 1, WIN):
                        n = dve.snap(passes)
                        dve.drain()
                        nc.vector.tensor_scalar(base[:], base[:], float(WIN), None, ALU.add)
                        dve.drain()
                        make_spread(c, h, base[:], more_spread)
                        add_window(n)
                dve.sem_inc(chunk_summed, 1)

            if weighted:
                dve.wait_ge(keep["y_in"], 16)
            dve.sem_inc(window_added, 1)
            if weighted:
                dve.sem_inc(parts_stored, 48)
                for c in range(RING):
                    stage_indices(nc.vector.tensor_copy, c, c)
                weigh(0, 0, 0)
            first_spread(0, 0)

            def normalise_node(tile):
                row = keep["rows"][:, bass.ds(tile, 1), :].rearrange("p t f -> p (t f)")
                dve.wait_ge(results_out, tile + 2)
                nc.vector.scalar_tensor_tensor(row, row, 2.0, relus[:], ALU.mult, ALU.add).then_inc(relus_used, 1)
                dve.drain()
                nc.vector.bn_stats(stats6[:], row)
                dve.drain()
                nc.vector.bn_aggr(moments[:], stats6[:])
                dve.drain()
                nc.vector.tensor_scalar(norm[:, 0:1], moments[:, 1:2], EPS, None, ALU.add).then_inc(var_ready, 1)
                dve.wait_ge(std_ready, tile + 1)
                nc.vector.reciprocal(norm[:, 2:3], norm[:, 1:2])
                dve.drain()
                nc.vector.scalar_tensor_tensor(norm[:, 3:4], moments[:, 0:1], -1.0, norm[:, 2:3], ALU.mult, ALU.mult)
                dve.drain()
                nc.vector.tensor_scalar(row, row, norm[:, 2:3], norm[:, 3:4], ALU.mult, ALU.add).then_inc(normed, 1)

            def step(c, i, h):
                if not is_last(c, 1):
                    if weighted:
                        weigh(c + 1, i, h + 1)
                    first_spread(c + 1, h + 1)
                sum_windows(c, h)
                if weighted and h == 0 and not is_last(c, RING):
                    dve.wait_ge(raw_in, i * 16 + 16)
                    dve.wait_ge(parts_stored, i * 48 + 48)
                    split_in_three(nc, dve, raw[:], rest[:], parts).then_inc(split, 1)
                if not weighted and h == 3:
                    if_ready(dve, i, begun, normalise_node)

            if not weighted:
                begun = node_counter(dve, "dve_begun")
                dve.sem_inc(relus_used, 1)
            over_chunks(dve, step)
            if not weighted:
                over_rest(dve, begun, normalise_node)


def close_layer_0(nc, io, keep):
    with ExitStack() as ctx:
        def sb(name, shape, dt=F32):
            return ctx.enter_context(nc.sbuf_tensor(name, shape, dt))

        def sem(name):
            return ctx.enter_context(nc.semaphore(name))

        x = keep["x"]
        ang = sb("ang", [P, NT])
        turns = sb("turns", [P, NT])
        below = sb("below", [P, NT])
        angles = sb("angles", [P, 2, NT])
        sines = sb("sines", [P, 2, NT])
        sine_attr = sb("sine_attr", [P, NT])
        stats6 = sb("row_stats6", [P, G, 6])
        stats2 = sb("row_stats2", [P, G, 2])
        stats = sb("row_stats", [P, NT, 2])
        norm = sb("row_norm", [P, 4, NT])
        mid_s = sb("mid_s", [MUL0, ROW])
        mid_v = sb("mid_v", [MUL1, 3, ROW])
        end_s = sb("end_s", [MUL0, MUL0])
        end_v = sb("end_v", [MUL1, MUL1])
        map1_scale = sb("map1_scale", [P, BLOCKS, 4])
        warm = sb("warm_root", [P, 1])
        mix_banks = ctx.enter_context(nc.psum_tensor("mix_banks", [P, 2, 512], F32))

        mids_in = sem("mids_in")
        mixed = sem("mixed")
        angles_ready = sem("angles_ready")
        sines_ready = sem("sines_ready")
        self_weighted = sem("self_weighted")
        var_ready = sem("row_var_ready")
        std_ready = sem("row_std_ready")
        shift_ready = sem("shift_ready")
        normed = sem("rows_normed")
        x1_stored = sem("x1_stored")
        block = ctx.enter_context(nc.Block())

        def row(place, n):
            return place[:, bass.ds(n, 1), :].rearrange("p t f -> p (t f)")

        def rows_of(place, g):
            return place[:, bass.ds(g * G, G), :].rearrange("p t f -> p (t f)")

        @block.sync
        def _(sp):
            for place, name in ((mid_s, "mid_s"), (mid_v, "mid_v"), (end_s, "end_s"), (end_v, "end_v"),
                                (map1_scale, "map1_scale")):
                sp.dma_start(place[:], io[name]).then_inc(mids_in, 16)
            with sp.Fori(0, NG) as g:
                sp.wait_ge(normed, g + 1)
                sp.dma_start(keep["x1_table"].rearrange("(t p) f -> p t f", p=P)[:, bass.ds(g * G, G), :],
                             keep["rows"][:, bass.ds(g * G, G), :]).then_inc(x1_stored, 16)
            sp.wait_ge(x1_stored, 16 * NG)

        @block.tensor
        def _(pe):
            pe.wait_ge(mids_in, 16 * 5)
            for k in range(BLOCKS):
                cols = slice(k * P, (k + 1) * P)
                pe.matmul(mix_banks[:, 0, k * MUL0:(k + 1) * MUL0], mid_s[:, cols], end_s[:], start=True, stop=True)
                for c in range(3):
                    at = (k * 3 + c) * MUL1
                    mm = pe.matmul(mix_banks[:, 1, at:at + MUL1], mid_v[:, c, cols], end_v[:], start=True, stop=True)
            mm.then_inc(mixed, 1)

        @block.scalar
        def _(act):
            act.wait_ge(angles_ready, 1)
            nc.scalar.activation(sines[:], angles[:], ACT.Sin).then_inc(sines_ready, 1)
            nc.scalar.activation(warm[:], keep["zeros"][:, 0:1], ACT.Sqrt)

            def root(g):
                act.wait_ge(var_ready, g + 1)
                at = bass.ds(g * G, G)
                nc.scalar.activation(norm[:, 1, at], norm[:, 0, at], ACT.Sqrt).then_inc(std_ready, 1)

            def normalise(g):
                act.wait_ge(shift_ready, g + 1)
                for t in range(G):
                    n = g * G + t
                    ins = nc.scalar.activation(row(keep["rows"], n), row(keep["rows"], n), ACT.Identity,
                                               bias=norm[:, 3, bass.ds(n, 1)], scale=norm[:, 2, bass.ds(n, 1)])
                ins.then_inc(normed, 1)

            def weigh_self(g):
                for t in range(G):
                    n = g * G + t
                    ins = nc.scalar.activation(row(keep["sc"], n), row(keep["sc"], n), ACT.Copy,
                                               scale=sines[:, 1, bass.ds(n, 1)])
                ins.then_inc(self_weighted, 1)

            act.wait_ge(sines_ready, 1)
            weigh_self(0)
            with act.Fori(0, NG - 1) as g:
                weigh_self(g + 1)
                root(g)
                normalise(g)
            root(NG - 1)
            normalise(NG - 1)

        @block.vector
        def _(dve):
            vv = nc.vector
            vv.tensor_tensor(ang[:], keep["angle"][:], keep["attr"][:], ALU.mult)
            dve.drain()
            vv.tensor_scalar(turns[:], ang[:], float(1 / TURN), ROUND, ALU.mult, ALU.add)
            dve.drain()
            vv.tensor_scalar(turns[:], turns[:], -ROUND, None, ALU.add)
            for part in (TURN_HI, TURN_MID, TURN_LO):
                dve.drain()
                vv.scalar_tensor_tensor(ang[:], turns[:], -part, ang[:], ALU.mult, ALU.add)
            dve.drain()
            vv.tensor_scalar(below[:], ang[:], float(np.pi / 2), float(-TURN), ALU.is_gt, ALU.mult)
            vv.tensor_scalar(angles[:, 1, :], ang[:], float(np.pi / 2), None, ALU.add)
            vv.tensor_scalar(angles[:, 0, :], ang[:], PI_IN, -PI_IN, ALU.min, ALU.max)
            dve.drain()
            vv.tensor_tensor(angles[:, 1, :], angles[:, 1, :], below[:], ALU.add)
            dve.drain()
            vv.tensor_scalar(angles[:, 1, :], angles[:, 1, :], PI_IN, -PI_IN, ALU.min,
                             ALU.max).then_inc(angles_ready, 1)
            dve.wait_ge(sines_ready, 1)
            vv.tensor_tensor(sine_attr[:], sines[:, 0, :], keep["attr"][:], ALU.mult)
            dve.drain()

            def add(g):
                for t in range(G):
                    n = g * G + t
                    vv.scalar_tensor_tensor(row(keep["rows"], n), row(keep["rows"], n), sine_attr[:, bass.ds(n, 1)],
                                            row(x, n), ALU.mult, ALU.add)
                dve.drain()
                dve.wait_ge(self_weighted, g + 1)
                vv.tensor_tensor(rows_of(keep["rows"], g), rows_of(keep["rows"], g), rows_of(keep["sc"], g), ALU.add)
                dve.drain()

            def take_stats(g):
                for t in range(G):
                    vv.bn_stats(stats6[:, t, :], row(keep["rows"], g * G + t))
                dve.drain()
                for t in range(G):
                    vv.bn_aggr(stats2[:, t, :], stats6[:, t, :])
                dve.drain()
                at = bass.ds(g * G, G)
                vv.tensor_copy(stats[:, at, :], stats2[:])
                vv.tensor_scalar(norm[:, 0, at], stats2[:, :, 1], EPS, None, ALU.add).then_inc(var_ready, 1)

            def make_shift(g):
                at = bass.ds(g * G, G)
                dve.wait_ge(std_ready, g + 1)
                vv.reciprocal(norm[:, 2, at], norm[:, 1, at])
                dve.drain()
                vv.scalar_tensor_tensor(norm[:, 3, at], stats[:, at, 0], -1.0, norm[:, 2, at],
                                        ALU.mult, ALU.mult).then_inc(shift_ready, 1)

            add(0)
            take_stats(0)
            with dve.Fori(0, NG - 1) as g:
                add(g + 1)
                make_shift(g)
                take_stats(g + 1)
            dve.wait_ge(mixed, 1)
            vv.tensor_tensor(keep["map1"][:, :, 0:MUL0],
                             mix_banks[:, 0, 0:BLOCKS * MUL0].rearrange("p (k f) -> p k f", k=BLOCKS),
                             map1_scale[:, :, 0:1].broadcast_to([P, BLOCKS, MUL0]), ALU.mult)
            vv.tensor_tensor(keep["map1"][:, :, MUL0:].rearrange("p k (c u) -> p k c u", c=3),
                             mix_banks[:, 1, 0:BLOCKS * 3 * MUL1].rearrange("p (k c u) -> p k c u", k=BLOCKS, c=3),
                             map1_scale[:, :, 1:].unsqueeze(3).broadcast_to([P, BLOCKS, 3, MUL1]), ALU.mult)
            make_shift(NG - 1)


def build(nc, io, out):
    with ExitStack() as ctx:
        def sb(name, shape, dt=F32):
            return ctx.enter_context(nc.sbuf_tensor(name, shape, dt))

        keep = {
            "rows": sb("rows", [P, NT, D]),
            "sc": sb("self_rows", [P, NT, D]),
            "x": sb("x_rows", [P, NT, D]),
            "angle": sb("angle", [P, NT]),
            "attr": sb("node_attr", [P, NT]),
            "src": sb("edge_src", [P, TILES + CH], I32),
            "dst": sb("edge_dst", [P, TILES]),
            "y": sb("edge_y", [P, TILES, NY]),
            "ranges": sb("ranges", [P, 2 * NCH], I32),
            "first_node": sb("first_node", [P, NCH]),
            "ready": sb("ready", [P, LOOPS], I32),
            "fc1": sb("fc1", [2 * K_HALF, 2 * HID], BF16),
            "fc2": sb("fc2", [2 * HID, WNUM]),
            "map0": sb("map0", [P, BLOCKS, OUTS[0]]),
            "map1": sb("map1", [P, BLOCKS, OUTS[1]]),
            "window_nodes": sb("window_nodes", [P, WIN]),
            "identity": sb("identity", [P, P]),
            "harmonic_mask": sb("harmonic_mask", [P, 2]),
            "zeros": sb("zeros", [P, PIECE // P * D]),
            "y_in": ctx.enter_context(nc.semaphore("y_in")),
            "early_zeros": ctx.enter_context(nc.semaphore("early_zeros")),
            "radial_parts": nc.dram_tensor("radial_parts", ((LOOPS + 1) * len(PAIRS) * P * SUB,), BF16,
                                           kind="Internal").ap(),
            "src_table": nc.dram_tensor("src_table", (NT * P, D), F32, kind="Internal").ap(),
            "x1_table": nc.dram_tensor("x1_table", (NT * P, D), F32, kind="Internal").ap(),
            "total0": nc.dram_tensor("total0", (TOTAL_ROWS, D), F32, kind="Internal").ap(),
            "total1": nc.dram_tensor("total1", (TOTAL_ROWS, D), F32, kind="Internal").ap(),
            "range_table": nc.dram_tensor("range_table", (1, 2 * NCH), I32, kind="Internal").ap(),
        }
        load_and_embed(nc, io, keep)
        sum_over_edges(nc, io, keep, 0)
        close_layer_0(nc, io, keep)
        sum_over_edges(nc, io, keep, 1, out)


def kernel(**inputs):
    import numpy as np
    import concourse.bacc as bacc
    from concourse.bass_utils import run_bass_kernel_spmd

    f = {name: np.asarray(a) for name, a in inputs.items()}

    def by_node(a):
        full = np.zeros((NT * P, a.shape[1]), a.dtype)
        full[:NODES] = a
        return np.ascontiguousarray(full.reshape(NT, P, -1).transpose(1, 0, 2))

    def by_edge(a, fill=0):
        full = np.full((EPAD, a.shape[1]), fill, a.dtype)
        full[:EDGES] = a
        return full

    def in_tiles(a):
        return np.ascontiguousarray(a.reshape(TILES, P, -1).transpose(1, 0, 2))

    def by_component(a):
        v = a[:, MUL0:].reshape(len(a), MUL1, 3).transpose(0, 2, 1)
        return np.concatenate([a[:, :MUL0], v.reshape(len(a), 3 * MUL1)], axis=1)

    def scalars(d):
        return slice(d * D, d * D + MUL0)

    def vectors(d, c):
        at = d * D + MUL0 + c * MUL1
        return slice(at, at + MUL1)

    def in_blocks(a):
        return np.ascontiguousarray(a.reshape(BLOCKS, P, -1).transpose(1, 0, 2))

    x, y = by_component(f["x"]), f["edge_attr_4"]
    x_t = np.zeros((D, NT * P), x.dtype)
    x_t[:, :NODES] = x.T
    embed = np.zeros((D, 2, D), x.dtype)
    for a, kind in enumerate(("W1", "W_sc")):
        embed[:MUL0, a, :MUL0] = f[f"L0_gnn_{kind}_s"]
        for c in range(3):
            embed[vectors(0, c), a, vectors(0, c)] = f[f"L0_gnn_{kind}_v"]
    map0 = np.zeros((ROW, OUTS[0]), x.dtype)
    map0_scale = np.full((ROW, 1), MIX / np.sqrt(NEIGHBORS), np.float32)
    mid_s = np.zeros((MUL0, ROW), x.dtype)
    mid_v = np.zeros((MUL1, 3, ROW), x.dtype)
    map1_scale = np.full((ROW, 4), C1 * LIN_V * INV3, np.float32)
    map1_scale[:, 0] = MIX * LIN_S
    map0[scalars(0), 0:1], map0[scalars(0), 1:1 + MUL0] = f["L0_gnn_W3"][:MUL0], f["L0_gnn_W2_s"][:MUL0]
    mid_s[:, scalars(0)] = f["L1_gnn_W1"].T
    for c in range(3):
        out = slice(1 + MUL0 + c * MUL1, 1 + MUL0 + (c + 1) * MUL1)
        a, b = (c + 1) % 3, (c + 2) % 3
        map0[vectors(1 + c, c), 0:1] = f["L0_gnn_W3"][MUL0:]
        map0[vectors(1 + c, c), 1:1 + MUL0] = f["L0_gnn_W2_s"][MUL0:]
        map0_scale[vectors(1 + c, c)] *= np.float32(INV3)
        map0[scalars(1 + c), out] = f["L0_gnn_W2_v"][:MUL0]
        map0[vectors(0, c), out] = f["L0_gnn_W2_v"][MUL0:]
        mid_s[:, vectors(1 + c, c)] = f["L1_gnn_W2"].T
        map1_scale[vectors(1 + c, c), 0] *= np.float32(INV3)
        mid_v[:, c, scalars(1 + c)] = f["L1_gnn_W3"].T
        mid_v[:, c, vectors(0, c)] = f["L1_gnn_W4"].T
        for d, comp, sign in ((b, a, 1.0), (a, b, -1.0)):
            mid_v[:, c, vectors(1 + d, comp)] = f["L1_gnn_W5"].T
            map1_scale[vectors(1 + d, comp), 1 + c] = sign * C1 * LIN_V * INV6
    fc1_rows = np.zeros((2, K_HALF, 2, HID), x.dtype)
    fc1_masks = np.zeros((2, TERMS, RAD, 3), np.float32)
    for half in range(2):
        fc1_rows[half, :, half] = np.tile(f["L0_gnn_fcW1"], (TERMS, 1))
    for t in range(TERMS):
        fc1_masks[:, t, :, PAIRS[t][1]] = 1.0
    radial = np.zeros((LOOPS + 1, P, SUB), x.dtype)
    radial[:LOOPS] = by_edge(f["edge_attr_8"]).T.reshape(RAD, LOOPS, P // RAD, SUB).transpose(1, 0, 2, 3).reshape(
        LOOPS, P, SUB)
    dst = by_edge(f["dst"].astype(np.int32)[:, None], f["dst"][-1])
    arrays = {
        "x": by_node(x),
        "x_t": x_t,
        "attr": by_node(f["node_vec1"])[:, :, 0].copy(),
        "src": np.pad(in_tiles(by_edge(f["src"].astype(np.int32)[:, None]))[:, :, 0], ((0, 0), (0, CH))),
        "dst": in_tiles(dst)[:, :, 0].copy(),
        "dst_chunks": dst.reshape(NCH // 2, 2, CHUNK),
        "y": in_tiles(by_edge(y)),
        "radial": radial,
        "embed_a": np.ascontiguousarray(embed[:P, :, :P]),
        "embed_b": np.ascontiguousarray(embed[P:, :, P:]),
        "fc1_rows": fc1_rows.reshape(P, 2 * HID),
        "fc1_masks": fc1_masks.reshape(P, 3),
        "fc2": np.concatenate([f["L0_gnn_fcW2"]] * 2),
        "map0": in_blocks(map0),
        "map0_scale": in_blocks(map0_scale),
        "map1_scale": in_blocks(map1_scale),
        "mid_s": mid_s,
        "mid_v": mid_v,
        "end_s": np.ascontiguousarray(f["L1_gnn_Ws"]),
        "end_v": np.ascontiguousarray(f["L1_gnn_Wv"]),
        "window_nodes": np.broadcast_to(np.arange(WIN, dtype=np.float32), (P, WIN)).copy(),
        "identity": np.eye(P, dtype=np.float32),
        "harmonic_mask": np.stack([np.arange(P) % NY == 0, np.arange(P) % NY != 0], axis=1).astype(np.float32),
    }

    nc = bacc.Bacc("TRN2", target_bir_lowering=False, num_devices=1)
    io = {name: nc.dram_tensor(f"in_{name}", a.shape, mybir.dt.from_np(a.dtype), kind="ExternalInput").ap()
          for name, a in arrays.items()}
    out = nc.dram_tensor("out_rows", (NT * P, D), F32, kind="ExternalOutput").ap()
    build(nc, io, out)
    run = run_bass_kernel_spmd(nc, [{f"in_{name}": a for name, a in arrays.items()}], core_ids=[0])
    rows = run.results[0]["out_rows"][:NODES]
    v = rows[:, MUL0:].reshape(NODES, 3, MUL1).transpose(0, 2, 1)
    return np.concatenate([rows[:, :MUL0], v.reshape(NODES, 3 * MUL1)], axis=1)
```
